# Optimizing a Trainium2 kernel written in Bass

```python
import numpy as np
import jax
import jax.numpy as jnp

def _softmax(x, axis=-1):
    return jax.nn.softmax(x, axis=axis)

def _gelu(x):
    return jax.nn.gelu(x, approximate=True)

def _silu(x):
    return jax.nn.silu(x)

def _sigmoid(x):
    return jax.nn.sigmoid(x)

def _layernorm(x, axis=-1, eps=1e-05):
    m = jnp.mean(x, axis=axis, keepdims=True)
    v = jnp.var(x, axis=axis, keepdims=True)
    return (x - m) / jnp.sqrt(v + eps)

def _scatter_add(tgt, idx, src, axis=0):
    return tgt.at[idx].add(src)

def _segment_sum(src, seg, n):
    return jax.ops.segment_sum(src, seg, n)
kernel_name = 'mk_seq_postln_d1_jaxref_r8_ed8a14'

def setup_inputs(seed: int=0):
    np.random.seed(seed)
    _w = jnp.asarray

    def _L0_attn_setup():
        import jax, jax.numpy as jnp
        import numpy as np
        H = 32
        KV = 8
        D = 128
        WINDOW = 128
        THETA = 10000.0

        def _rope_tables(seq_len, dtype=jnp.float32):
            inv_freq = 1.0 / THETA ** (jnp.arange(0, D, 2, dtype=jnp.float32) / D)
            t = jnp.arange(seq_len, dtype=jnp.float32)
            freqs = t[:, None] * inv_freq[None, :]
            emb = jnp.concatenate([freqs, freqs], axis=-1)
            return (jnp.cos(emb).astype(dtype), jnp.sin(emb).astype(dtype))

        def _rotate_half(x):
            x1, x2 = (x[..., :D // 2], x[..., D // 2:])
            return jnp.concatenate([-x2, x1], axis=-1)
        key = jax.random.key(seed)
        ks = jax.random.split(key, 5)
        B, S, E = (1, 256, 512)
        sc = 0.02
        return {'hidden_states': jax.random.normal(ks[0], (B, S, E), jnp.float32), 'Wq': jax.random.normal(ks[1], (H * D, E), jnp.float32) * sc, 'Wk': jax.random.normal(ks[2], (KV * D, E), jnp.float32) * sc, 'Wv': jax.random.normal(ks[3], (KV * D, E), jnp.float32) * sc, 'Wo': jax.random.normal(ks[4], (E, H * D), jnp.float32) * sc}
    _L0_attn_in = _L0_attn_setup()

    def _L0_ffn_setup():
        import jax, jax.numpy as jnp
        import numpy as np

        def sparsemax(z):
            E = z.shape[-1]
            z_sorted = -jnp.sort(-z, axis=-1)
            z_cum = jnp.cumsum(z_sorted, axis=-1)
            k = jnp.arange(1, E + 1, dtype=z.dtype)
            support = 1.0 + k * z_sorted > z_cum
            k_z = jnp.sum(support, axis=-1, keepdims=True)
            tau_sum = jnp.take_along_axis(z_cum, k_z.astype(jnp.int32) - 1, axis=-1)
            tau = (tau_sum - 1.0) / k_z.astype(z.dtype)
            return jnp.maximum(z - tau, 0.0)
        key = jax.random.key(seed)
        ks = jax.random.split(key, 6)
        B, S, D_IN, D_OUT, E, R = (8, 256, 512, 512, 8, 16)
        x = jax.random.normal(ks[0], (B, S, D_IN), dtype=jnp.float32)
        W_base = jax.random.normal(ks[1], (D_OUT, D_IN), dtype=jnp.float32) * D_IN ** (-0.5)
        b_base = jax.random.normal(ks[2], (D_OUT,), dtype=jnp.float32) * 0.01
        W_router = jax.random.normal(ks[3], (E, D_IN), dtype=jnp.float32) * D_IN ** (-0.5)
        b_router = jnp.zeros((E,), dtype=jnp.float32)
        lora_A = jax.random.normal(ks[4], (E, D_IN, R), dtype=jnp.float32) * D_IN ** (-0.5)
        lora_B = jnp.zeros((E, R, D_OUT), dtype=jnp.float32)
        return {'x': x, 'W_base': W_base, 'b_base': b_base, 'W_router': W_router, 'b_router': b_router, 'lora_A': lora_A, 'lora_B': lora_B}
    _L0_ffn_in = _L0_ffn_setup()
    _d = {'L0_attn_hidden_states': _L0_attn_in['hidden_states'], 'L0_attn_Wq': _L0_attn_in['Wq'], 'L0_attn_Wk': _L0_attn_in['Wk'], 'L0_attn_Wv': _L0_attn_in['Wv'], 'L0_attn_Wo': _L0_attn_in['Wo'], 'L0_ffn_W_base': _L0_ffn_in['W_base'], 'L0_ffn_b_base': _L0_ffn_in['b_base'], 'L0_ffn_W_router': _L0_ffn_in['W_router'], 'L0_ffn_b_router': _L0_ffn_in['b_router'], 'L0_ffn_lora_A': _L0_ffn_in['lora_A'], 'L0_ffn_lora_B': _L0_ffn_in['lora_B']}
    _x0 = _d['L0_attn_hidden_states']
    _d['L0_attn_hidden_states'] = jax.random.normal(jax.random.fold_in(jax.random.key(seed), 1), (2, 1024, 512), dtype=_x0.dtype)
    del _x0
    return _d

def reference(L0_attn_hidden_states, L0_attn_Wq, L0_attn_Wk, L0_attn_Wv, L0_attn_Wo, L0_ffn_W_base, L0_ffn_b_base, L0_ffn_W_router, L0_ffn_b_router, L0_ffn_lora_A, L0_ffn_lora_B):

    def _L0_attn_ref(hidden_states, Wq, Wk, Wv, Wo):
        import jax, jax.numpy as jnp
        import numpy as np
        H = 32
        KV = 8
        D = 128
        WINDOW = 128
        THETA = 10000.0

        def _rope_tables(seq_len, dtype=jnp.float32):
            inv_freq = 1.0 / THETA ** (jnp.arange(0, D, 2, dtype=jnp.float32) / D)
            t = jnp.arange(seq_len, dtype=jnp.float32)
            freqs = t[:, None] * inv_freq[None, :]
            emb = jnp.concatenate([freqs, freqs], axis=-1)
            return (jnp.cos(emb).astype(dtype), jnp.sin(emb).astype(dtype))

        def _rotate_half(x):
            x1, x2 = (x[..., :D // 2], x[..., D // 2:])
            return jnp.concatenate([-x2, x1], axis=-1)
        B, S, E = hidden_states.shape
        q = (hidden_states @ Wq.T).reshape(B, S, H, D).transpose(0, 2, 1, 3)
        k = (hidden_states @ Wk.T).reshape(B, S, KV, D).transpose(0, 2, 1, 3)
        v = (hidden_states @ Wv.T).reshape(B, S, KV, D).transpose(0, 2, 1, 3)
        cos, sin = _rope_tables(S, hidden_states.dtype)
        cos = cos[None, None]
        sin = sin[None, None]
        q = q * cos + _rotate_half(q) * sin
        k = k * cos + _rotate_half(k) * sin
        k = jnp.repeat(k, H // KV, axis=1)
        v = jnp.repeat(v, H // KV, axis=1)
        scores = jnp.einsum('bhqd,bhkd->bhqk', q, k) / jnp.sqrt(jnp.asarray(D, q.dtype))
        i = jnp.arange(S)[:, None]
        j = jnp.arange(S)[None, :]
        band = jnp.abs(i - j) < WINDOW
        scores = jnp.where(band[None, None], -jnp.inf, scores)
        attn = jax.nn.softmax(scores, axis=-1)
        out = jnp.einsum('bhqk,bhkd->bhqd', attn, v)
        out = out.transpose(0, 2, 1, 3).reshape(B, S, H * D)
        return out @ Wo.T

    def _L0_ffn_ref(x, W_base, b_base, W_router, b_router, lora_A, lora_B):
        import jax, jax.numpy as jnp
        import numpy as np

        def sparsemax(z):
            E = z.shape[-1]
            z_sorted = -jnp.sort(-z, axis=-1)
            z_cum = jnp.cumsum(z_sorted, axis=-1)
            k = jnp.arange(1, E + 1, dtype=z.dtype)
            support = 1.0 + k * z_sorted > z_cum
            k_z = jnp.sum(support, axis=-1, keepdims=True)
            tau_sum = jnp.take_along_axis(z_cum, k_z.astype(jnp.int32) - 1, axis=-1)
            tau = (tau_sum - 1.0) / k_z.astype(z.dtype)
            return jnp.maximum(z - tau, 0.0)
        base_out = jnp.einsum('bsd,od->bso', x, W_base) + b_base
        logits = jnp.einsum('bsd,ed->bse', x, W_router) + b_router
        weights = sparsemax(logits)
        h = jnp.einsum('bsd,edr->bser', x, lora_A)
        expert_out = jnp.einsum('bser,bse,ero->bso', h, weights, lora_B)
        return base_out + expert_out
    x = L0_attn_hidden_states
    x = _layernorm(x + _L0_attn_ref(x, L0_attn_Wq, L0_attn_Wk, L0_attn_Wv, L0_attn_Wo), axis=-1)
    x = _layernorm(x + _L0_ffn_ref(x, L0_ffn_W_base, L0_ffn_b_base, L0_ffn_W_router, L0_ffn_b_router, L0_ffn_lora_A, L0_ffn_lora_B), axis=-1)
    return x

_drawn_inputs = setup_inputs


def setup_inputs(seed=0):
    import zlib

    import numpy as np

    out = dict(_drawn_inputs(seed))
    spreads = {'L0_ffn_b_router': (0.0, 0.524), 'L0_ffn_lora_B': (0.0, 0.1)}
    factors = {'L0_attn_Wq': 8.0,
     'L0_attn_Wk': 8.0,
     'L0_attn_Wv': 2.724,
     'L0_attn_Wo': 2.689,
     'L0_ffn_b_base': 8.0}
    for name, (base, spread) in spreads.items():
        noise = np.random.default_rng([zlib.crc32(name.encode()), seed]).standard_normal(out[name].shape)
        drawn = base * np.exp(spread * noise) if base else spread * noise
        out[name] = jnp.asarray(drawn.astype(out[name].dtype))
    for name, factor in factors.items():
        out[name] = (out[name] * factor).astype(out[name].dtype)
    return out
```

```python
from contextlib import ExitStack

import concourse.bass as bass
from concourse import mybir
from concourse.alu_op_type import AluOpType as ALU

ACT = mybir.ActivationFunctionType
AX = mybir.AxisListType
F32 = mybir.dt.float32
F32R = mybir.dt.float32r
BF16 = mybir.dt.bfloat16

P = 128
HEADS_PER_KV = 4
EPS = 1e-5
MASKED = -3.0e38


def score_chunks(i, tiles):
    first_bank = 3 if i in (2, 4) else 4
    start = (4 - first_bank) * P
    cuts = {0: [4, 3], 1: [4, 3], 2: [3, 2, 2], 3: [4, 3], 4: [3, 4], 5: [2, 2, 3], 6: [2, 2, 3], 7: [4, 3]}[i]
    chunks, t = [], 0
    for n in cuts:
        block = (i + 1 + t) % tiles
        assert block + n <= tiles + 1
        chunks.append((start + t * P, block, n))
        t += n
    assert t == tiles - 1
    return start, chunks


def attention_ffn(nc, xT, x, wqT, wkvT, woT, loraB, b_base, b_router, cosT, sinT, ranks, out):
    B, S, E = x.shape
    KV = woT.shape[0]
    H = HEADS_PER_KV
    D = wkvT.shape[2] // 2
    C = E // P
    T = S // P
    TV = T - 1
    KEYS = TV * P
    R = loraB.shape[0]
    NEXP = b_router.shape[0]
    RANK = R // NEXP
    HP = H * P
    SCALE = float(D) ** -0.5
    assert D == P and R == P and T == 8 and C == 4 and H == 4 and E == 512

    ctx = ExitStack()
    with ctx:
        def sb(name, shape, dt=F32):
            return ctx.enter_context(nc.sbuf_tensor(name, shape, dt))

        def sem(name):
            return ctx.enter_context(nc.semaphore(name))

        x_hi = sb("x_hi", [P, C, S], F32R)
        x_lo = sb("x_lo", [P, C, S], F32R)
        y = sb("y", [P, T, E])
        k_hi = sb("k_hi", [P, (T + 1) * P], F32R)
        k_lo = sb("k_lo", [P, (T + 1) * P], F32R)
        k_next = sb("k_next", [P, S])
        v_hi = sb("v_hi", [P, T, D], F32R)
        v_lo = sb("v_lo", [P, T, D], F32R)
        v_next = sb("v_next", [P, T, D])
        vT = sb("vT", [P, 4 * P])
        q_hi = sb("q_hi", [P, 2, H, 2 * P], F32R)
        q_lo = sb("q_lo", [P, 2, H, 2 * P], F32R)
        p = sb("p", [P, 2, H, KEYS])
        pT_hi = sb("pT_hi", [P, 2, HP], F32R)
        pT_lo = sb("pT_lo", [P, 2, HP], F32R)
        oT_hi = sb("oT_hi", [P, HP], F32R)
        oT_lo = sb("oT_lo", [P, HP], F32R)
        wq_hi = sb("wq_hi", [P, C, HP], F32R)
        wq_lo = sb("wq_lo", [P, C, HP], F32R)
        wkv_hi = sb("wkv_hi", [P, C, 2 * D], F32R)
        wkv_lo = sb("wkv_lo", [P, C, 2 * D], F32R)
        wo_hi = sb("wo_hi", [P, H, E], F32R)
        wo_lo = sb("wo_lo", [P, H, E], F32R)
        lb_hi = sb("lb_hi", [P, E], F32R)
        lb_lo = sb("lb_lo", [P, E], F32R)
        stage = [sb(f"stage{i}", [P, 2 * HP]) for i in range(2)]
        rope_a = sb("rope_a", [P, 2 * 2 * P])
        rope_s = sb("rope_s", [P, 2 * 2 * P])
        cos_sb = sb("cos_sb", [P, S])
        sin_sb = sb("sin_sb", [P, S])
        mask_mid = sb("mask_mid", [P, KEYS], BF16)
        mask_end = sb("mask_end", [P, KEYS + P], BF16)
        ident = sb("ident", [P, P])
        row_max = sb("row_max", [P, 2, H])
        neg_max = sb("neg_max", [P, 2, H])
        row_sum = sb("row_sum", [P, 2, H])
        row_inv = sb("row_inv", [P, 2, H])
        h_sb = sb("h_sb", [P, T, R + NEXP])
        bb = sb("bb", [P, E])
        small = sb("small", [P, 3 * T + 2 * NEXP + 4])
        stats = sb("stats", [P, T, 6])
        mv = sb("mv", [P, T, 2])
        std = sb("std", [P, T])
        rstd = sb("rstd", [P, T])
        mv2 = sb("mv2", [P, T, 2])
        std2 = sb("std2", [P, T])
        rstd2 = sb("rstd2", [P, T])
        z = sb("z", [P, T, NEXP])
        zs = sb("zs", [P, T, NEXP])
        zc = sb("zc", [P, T, NEXP])
        zk = sb("zk", [P, T, NEXP])
        zt = sb("zt", [P, T, NEXP])
        wts = sb("wts", [P, T, NEXP])
        kz, tau, rk = (small[:, i * T:(i + 1) * T] for i in range(3))
        br = small[:, 3 * T:3 * T + NEXP]
        rank = small[:, 3 * T + NEXP:3 * T + 2 * NEXP]
        eps = small[:, 3 * T + 2 * NEXP:3 * T + 2 * NEXP + 1]

        ps_s = ctx.enter_context(nc.psum_tensor("ps_s", [P, 2, 1024], F32))
        ps_t = ctx.enter_context(nc.psum_tensor("ps_t", [P, 2, 512], F32))
        ps_o = ctx.enter_context(nc.psum_tensor("ps_o", [P, 512], F32))
        ps_m = ctx.enter_context(nc.psum_tensor("ps_m", [P, 512], F32))

        x_raw = p[:, :, :, :].rearrange("p a h k -> p (a h k)")

        consts_in = sem("consts_in")
        waits_passed = sem("waits_passed")
        built = sem("built")
        xt_in = [sem(f"xt_in{c}") for c in range(C)]
        y_in = sem("y_in")
        stage_in = [sem("stage_in0"), sem("stage_in1")]
        stage1_free = sem("stage1_free")
        wkv_split, wq_split, wo_split = sem("wkv_split"), sem("wq_split"), sem("wo_split")
        lb_split = sem("lb_split")
        w_hi_done = sem("w_hi_done")
        xh_done = sem("xh_done")
        xl_done = sem("xl_done")
        proj_ready = sem("proj_ready")
        half_swapped = sem("half_swapped")
        rope_cos, rope_swapped, rope_sin, rope_sum = (sem("rope_cos"), sem("rope_swapped"), sem("rope_sin"), sem("rope_sum"))
        q_hi_done, q_split = sem("q_hi_done"), sem("q_split")
        k_hi_done, k_split = sem("k_hi_done"), sem("k_split")
        v_proj, vT_copied, v_turned, v_copied = sem("v_proj"), sem("vT_copied"), sem("v_turned"), sem("v_copied")
        v_used = sem("v_used")
        v_hi_done, v_split = sem("v_hi_done"), sem("v_split")
        s_ready = sem("s_ready")
        masked = sem("masked")
        negated = sem("negated")
        exp_done = sem("exp_done")
        inverted = sem("inverted")
        normed = sem("normed")
        pT_ready = sem("pT_ready")
        pT_hi_done, pT_split = sem("pT_hi_done"), sem("pT_split")
        o_ready = sem("o_ready")
        oT_hi_done, oT_split = sem("oT_hi_done"), sem("oT_split")
        wo_ready = sem("wo_ready")
        y_added = sem("y_added")
        chain = sem("chain")
        f_stat, f_std, f_rstd, f_norm = sem("f_stat"), sem("f_std"), sem("f_rstd"), sem("f_norm")
        f_turned, f_hi, f_lo, f_h, f_copied = (sem("f_turned"), sem("f_hi"), sem("f_lo"), sem("f_h"), sem("f_copied"))
        f_stats = sem("f_stats")
        f_biased = sem("f_biased")
        f_gated, f_gT, f_gT_hi, f_gT_lo = sem("f_gated"), sem("f_gT"), sem("f_gT_hi"), sem("f_gT_lo")
        f_out, f_sum, f_stat2, f_std2, f_rstd2, f_done = (sem("f_out"), sem("f_sum"), sem("f_stat2"), sem("f_std2"), sem("f_rstd2"), sem("f_done"))
        stored = sem("stored")

        def rope_slot(g, what, last):
            order = []
            for gg in range(T):
                if not last or gg <= 4:
                    order.append((gg, "q"))
                if not last and gg in (1, 2):
                    order.append((gg, "k"))
            return 5 + order.index((g, what))

        CREDIT = 2
        gated = vT[:, 0:2 * P].rearrange("p (a n) -> p a n", a=2)

        block = ctx.enter_context(nc.Block())

        def counts(eng, b, kv):
            n = b * KV + kv
            held = {k: eng.snap(n * k) for k in (1, 2, 5, 8, 10, T * H, T * TV)}
            held["nb"] = eng.snap(n + b)

            def after(dn):
                def at(k, c):
                    return held[k] + ((dn if k == "nb" else dn * k) + c)
                return at
            return after

        def wait_apart(eng, s, count):
            eng.wait_ge(s, count)
            eng.sem_inc(waits_passed, 1)

        def tiles_of_batch(eng, b, tile):
            after = counts(eng, b, 0)
            tile(0, after(0), last=False, first=True)
            with eng.Fori(0, KV - 1) as kv:
                after = counts(eng, b, kv)
                for g in range(1, T):
                    tile(g, after(0), last=False)
                tile(0, after(1), last=False)
            after = counts(eng, b, KV - 1)
            for g in range(1, T):
                tile(g, after(0), last=True)

        def following(g):
            return (1, 0) if g == T - 1 else (0, g + 1)

        @block.sync
        def _(sp):
            sp.dma_start(cos_sb[:], cosT).then_inc(consts_in, 16)
            sp.dma_start(sin_sb[:], sinT).then_inc(consts_in, 16)
            sp.dma_start(rank, ranks.rearrange("(a n) -> a n", a=1).broadcast_to([P, NEXP])).then_inc(consts_in, 16)
            sp.dma_start(br, b_router.rearrange("(a n) -> a n", a=1).broadcast_to([P, NEXP])).then_inc(consts_in, 16)
            sp.dma_start(bb[:], b_base.rearrange("(a n) -> a n", a=1).broadcast_to([P, E])).then_inc(consts_in, 16)

            def load(i, src):
                sp.dma_start(stage[i][:].rearrange("p (c n) -> p c n", c=src.shape[1]), src).then_inc(stage_in[i], 16)

            def of_group(w, kv):
                return w[bass.ds(kv, 1)].rearrange("a (c p) n -> p (a c) n", p=P)

            with sp.Fori(0, B) as b:
                for c in range(C):
                    sp.dma_start(x_raw[:, c * S:(c + 1) * S],
                                 xT[bass.ds(b, 1), c * P:(c + 1) * P, :].rearrange("a p s -> (a p) s"))\
                        .then_inc(xt_in[c], 16)
                load(0, of_group(wkvT, 0))
                load(1, of_group(wqT, 0)[:, 0:2])
                sp.wait_ge(wkv_split, b * (KV + 1) + 1)
                load(0, of_group(wqT, 0)[:, 2:4])
                sp.dma_start(y[:], x[bass.ds(b, 1)].rearrange("a (t p) e -> p (a t) e", p=P)).then_inc(y_in, 16)
                with sp.Fori(0, KV) as kv:
                    nb, n2b = b * (KV + 1) + kv, b * (2 * KV + 1) + kv * 2
                    sp.wait_ge(wq_split, nb + 1)
                    load(0, of_group(wkvT, kv + 1))
                    sp.wait_ge(stage1_free, n2b + 1)
                    load(1, of_group(woT, kv)[:, 0:2])
                    sp.wait_ge(wkv_split, nb + 2)
                    load(0, of_group(woT, kv)[:, 2:4])
                    sp.wait_ge(stage1_free, n2b + 2)
                    load(1, of_group(wqT, kv + 1)[:, 0:2])
                    sp.wait_ge(wo_split, b * KV + kv + 1)
                    load(0, of_group(wqT, kv + 1)[:, 2:4])
                sp.wait_ge(stage1_free, (b + 1) * (2 * KV + 1))
                sp.dma_start(stage[1][:, 0:E], loraB).then_inc(stage_in[1], 16)
                for i in range(T):
                    sp.wait_ge(f_done, b * T + i + 1)
                    sp.dma_start(out[bass.ds(b, 1), i * P:(i + 1) * P, :].rearrange("a s e -> (a s) e"),
                                 y[:, i, :]).then_inc(stored, 16)
                wait_apart(sp, stored, (b + 1) * (16 * T))

        @block.gpsimd
        def _(pool):
            nc.gpsimd.memset(ident[:], 0.0).then_inc(built, 1)
            nc.gpsimd.memset(mask_mid[:], 0.0).then_inc(built, 1)
            nc.gpsimd.memset(mask_end[:], 0.0).then_inc(built, 1)
            nc.gpsimd.memset(eps, EPS).then_inc(built, 1)
            pool.wait_ge(built, 4)
            nc.gpsimd.affine_select(out=ident[:], in_=ident[:], compare_op=ALU.not_equal, fill=1.0, base=0,
                                    pattern=[[-1, P]], channel_multiplier=1).then_inc(built, 1)
            for m, end in ((mask_mid, KEYS), (mask_end, KEYS + P)):
                nc.gpsimd.affine_select(out=m[:, 0:P], in_=m[:, 0:P], compare_op=ALU.is_ge, fill=MASKED, base=0,
                                        pattern=[[1, P]], channel_multiplier=-1).then_inc(built, 1)
                nc.gpsimd.affine_select(out=m[:, end - P:end], in_=m[:, end - P:end], compare_op=ALU.is_ge,
                                        fill=MASKED, base=0, pattern=[[-1, P]],
                                        channel_multiplier=1).then_inc(built, 1)

            def split(i, loaded, hi, lo, width, hi_count):
                wait_apart(pool, stage_in[i], loaded)
                src = stage[i][:, 0:width]
                nc.gpsimd.tensor_scalar(hi, src, 1.0, 1.0, ALU.mult, ALU.mult).then_inc(w_hi_done, 1)
                pool.wait_ge(w_hi_done, hi_count)
                return nc.gpsimd.tensor_tensor(lo, src, hi.bitcast(F32), ALU.subtract)

            def chunks(t, a=0, z_=C):
                return t[:, a:z_].rearrange("p c n -> p (c n)")

            def norm(at, dn, j, h):
                wait_apart(pool, inverted, at(T * H, dn * T * H + j * H + h + 1))
                nc.gpsimd.tensor_scalar(p[:, j % 2, h, :], p[:, j % 2, h, :], row_inv[:, j % 2, h:h + 1], 1.0,
                                        ALU.mult, ALU.mult).then_inc(normed, 1)

            def times_sin(at, r, t0, tokens, heads):
                pool.wait_ge(rope_swapped, at(10, r + 1))
                s = rope_s[:].rearrange("p (h t) -> p h t", h=heads)
                sn = sin_sb[:, t0:t0 + tokens].unsqueeze(1).broadcast_to([P, heads, tokens])
                nc.gpsimd.tensor_tensor(s, s, sn, ALU.mult).then_inc(rope_sin, 1)

            with pool.Fori(0, B) as b:
                hi0 = pool.snap(b * (5 * KV + 4))
                in0, in1 = pool.snap(b * (16 * (3 * KV + 2))), pool.snap(b * (16 * (2 * KV + 2)))
                split(0, in0 + 16, chunks(wkv_hi), chunks(wkv_lo), 2 * HP, hi0 + 1).then_inc(wkv_split, 1)
                split(1, in1 + 16, chunks(wq_hi, 0, 2), chunks(wq_lo, 0, 2), 2 * HP, hi0 + 2)\
                    .then_inc(stage1_free, 1)
                split(0, in0 + 32, chunks(wq_hi, 2, 4), chunks(wq_lo, 2, 4), 2 * HP, hi0 + 3)\
                    .then_inc(wq_split, 1)
                pool.wait_ge(consts_in, 16 * 5)
                at0 = counts(pool, b, 0)(0)
                times_sin(at0, 0, 0, 512, 1)
                times_sin(at0, 1, 512, 512, 1)
                times_sin(at0, 2, 0, 2 * P, 2)
                times_sin(at0, 3, 0, 2 * P, 2)
                times_sin(at0, 4, 2 * P, 2 * P, 2)
                for h in range(H):
                    norm(at0, 0, 0, h)

                b4, b2_16 = pool.snap(b * 4), pool.snap(b * 32)

                def tile(g, at, last, first=False):
                    dn, j = following(g)
                    if g == 0:
                        pool.wait_ge(v_proj, at(2, 2))
                        split(0, at(2, 0) * 16 + at(1, 0) * 16 + b2_16 + 16 * 3, chunks(wkv_hi), chunks(wkv_lo),
                              2 * HP, at(5, 4) + b4).then_inc(wkv_split, 1)
                    if not last and g in (2, 3):
                        times_sin(at, rope_slot(g - 1, "k", last), (g - 2) * 512, 512, 1)
                    if not (last and g == T - 1):
                        for h in range(H):
                            norm(at, dn, j, h)
                    if not last or g <= 4:
                        times_sin(at, rope_slot(g, "q", last), ((g + 3) // 2) % 4 * 2 * P, 2 * P, 2)
                    if g == 0:
                        if not first:
                            pool.wait_ge(wo_ready, at(8, 0))
                        split(1, at(2, 2) * 16 + b2_16, chunks(wo_hi, 0, 2), chunks(wo_lo, 0, 2), 2 * HP,
                              at(5, 5) + b4).then_inc(stage1_free, 1)
                        split(0, at(2, 0) * 16 + at(1, 0) * 16 + b2_16 + 16 * 4, chunks(wo_hi, 2, 4),
                              chunks(wo_lo, 2, 4), 2 * HP, at(5, 6) + b4).then_inc(wo_split, 1)
                    if g == 4:
                        pool.wait_ge(proj_ready, at(10, rope_slot(4, "q", last) + 1))
                        split(1, at(2, 3) * 16 + b2_16, chunks(wq_hi, 0, 2), chunks(wq_lo, 0, 2), 2 * HP,
                              at(5, 7) + b4).then_inc(stage1_free, 1)
                        split(0, at(2, 0) * 16 + at(1, 0) * 16 + b2_16 + 16 * 5, chunks(wq_hi, 2, 4),
                              chunks(wq_lo, 2, 4), 2 * HP, at(5, 8) + b4).then_inc(wq_split, 1)

                tiles_of_batch(pool, b, tile)
                split(1, (b + 1) * (16 * (2 * KV + 2)), lb_hi[:], lb_lo[:], E, (b + 1) * (5 * KV + 4))\
                    .then_inc(lb_split, 1)
                for i in range(T):
                    pool.wait_ge(f_turned, b * T + i + 1)
                    nc.gpsimd.tensor_tensor(y[:, i, :], y[:, i, :], bb[:], ALU.add).then_inc(f_biased, 1)
                pool.wait_ge(f_out, (b + 1) * T)

        @block.tensor
        def _(pe):
            def three(out_, a_hi, a_lo, b_hi, b_lo, first, last):
                nc.tensor.matmul(out_, a_hi, b_hi, start=first, stop=False)
                nc.tensor.matmul(out_, a_hi, b_lo, start=False, stop=False)
                return nc.tensor.matmul(out_, a_lo, b_hi, start=False, stop=last)

            def project_q(bank, pair, half):
                t0 = pair * 2 * P
                for hh in range(2):
                    h = 2 * half + hh
                    for c in range(C):
                        mm = three(bank[:, hh * 2 * P:(hh + 1) * 2 * P], wq_hi[:, c, h * P:(h + 1) * P],
                                   wq_lo[:, c, h * P:(h + 1) * P], x_hi[:, c, t0:t0 + 2 * P],
                                   x_lo[:, c, t0:t0 + 2 * P], c == 0, c == C - 1)
                mm.then_inc(proj_ready, 1)

            def project_kv(bank, which, half):
                w, t0 = which * D, half * 512
                for c in range(C):
                    mm = three(bank, wkv_hi[:, c, w:w + D], wkv_lo[:, c, w:w + D], x_hi[:, c, t0:t0 + 512],
                               x_lo[:, c, t0:t0 + 512], c == 0, c == C - 1)
                mm.then_inc(v_proj if which else proj_ready, 1)

            def turn_v(bank):
                for k in range(4):
                    mm = nc.tensor.transpose(bank[:, k * P:(k + 1) * P], vT[:, k * P:(k + 1) * P], ident[:])
                mm.then_inc(v_turned, 1)

            def scores(at, dn, j, h, fresh=False):
                if h == 0 and j == 0:
                    pe.wait_ge(k_split, at(1, dn + 1))
                if j % 2 == 0 and h % 2 == 0:
                    pe.wait_ge(q_split, at(8, dn * 8 + j + h // 2 + 1))
                if not (fresh and h < 2):
                    pe.wait_ge(masked, at(T * H, dn * T * H + j * H + h - 1))
                slot, off = h % 2, (j % 2) * P
                for col, kb, cnt in score_chunks(j, T)[1]:
                    mm = three(ps_s[:, slot, col:col + cnt * P],
                               q_hi[:, (j // 2) % 2, h, off:off + P], q_lo[:, (j // 2) % 2, h, off:off + P],
                               k_hi[:, kb * P:(kb + cnt) * P], k_lo[:, kb * P:(kb + cnt) * P], True, True)
                mm.then_inc(s_ready, 1)

            def turn_p(at, g, t):
                if t == 0:
                    pe.wait_ge(normed, at(T * H, (g + 1) * H))
                k = g * TV + t
                pe.wait_ge(pT_split, at(T * TV, k - 1 + CREDIT))
                for h in range(H):
                    mm = nc.tensor.transpose(ps_t[:, k % 2, h * P:(h + 1) * P], p[:, g % 2, h, t * P:(t + 1) * P],
                                             ident[:])
                mm.then_inc(pT_ready, 1)

            def times_v(at, g, t, first=False):
                k, j = g * TV + t, (g + 1 + t) % T
                if t == 0 and not first:
                    pe.wait_ge(oT_split, at(8, g))
                if g == 0 and t in (0, 3):
                    pe.wait_ge(v_split, at(2, 1 if t == 0 else 2))
                pe.wait_ge(pT_split, at(T * TV, k + 1 + CREDIT))
                mm = three(ps_o[:], v_hi[:, j, :], v_lo[:, j, :], pT_hi[:, k % 2, :], pT_lo[:, k % 2, :],
                           t == 0, t == TV - 1)
                if t == TV - 1:
                    mm.then_inc(o_ready, 1)
                elif g == T - 1 and t == 3:
                    mm.then_inc(v_used, 1)

            def times_wo(at, g):
                pe.wait_ge(oT_split, at(8, g))
                if g == 1:
                    pe.wait_ge(wo_split, at(1, 1))
                for h in range(H):
                    mm = three(ps_m[:], oT_hi[:, h * P:(h + 1) * P], oT_lo[:, h * P:(h + 1) * P],
                               wo_hi[:, h, :], wo_lo[:, h, :], h == 0, h == H - 1)
                mm.then_inc(wo_ready, 1)

            def projections_read(at, g, last):
                if g == 0:
                    pe.wait_ge(rope_swapped, at(10, 5))
                elif last and g >= 6:
                    pe.wait_ge(y_added, at(8, g - 1))
                elif not last and g in (2, 3):
                    pe.wait_ge(rope_swapped, at(10, rope_slot(g - 1, "k", last) + 1))
                elif not last and g in (4, 6):
                    pe.wait_ge(vT_copied, at(2, 3 if g == 4 else 4))
                elif not last and g in (5, 7):
                    pe.wait_ge(v_copied, at(2, 3 if g == 5 else 4))
                else:
                    pe.wait_ge(rope_swapped, at(10, rope_slot(g - 1, "q", last) + 1))

            def tile(g, at, last, first=False):
                dn, j = following(g)
                more = not (last and g == T - 1)
                turn_p(at, g, 0)
                turn_p(at, g, 1)
                if more:
                    scores(at, dn, j, 0)
                times_v(at, g, 0, first)
                turn_p(at, g, 2)
                if more:
                    scores(at, dn, j, 1)
                projections_read(at, g, last)
                if not first:
                    times_wo(at, g)
                times_v(at, g, 1)
                turn_p(at, g, 3)
                if more:
                    scores(at, dn, j, 2)
                times_v(at, g, 2)
                turn_p(at, g, 4)
                if more:
                    scores(at, dn, j, 3)
                if not last or g <= 4:
                    if g == 5:
                        pe.wait_ge(wq_split, at("nb", 2))
                    if not first:
                        pe.wait_ge(y_added, at(8, g))
                    project_q(ps_m[:], ((g + 3) // 2) % 4, (g + 1) % 2)
                times_v(at, g, 3)
                turn_p(at, g, 5)
                times_v(at, g, 4)
                turn_p(at, g, 6)
                times_v(at, g, 5)
                if not last and 1 <= g <= 6:
                    pe.wait_ge(rope_swapped, at(10, rope_slot(g, "q", last) + 1))
                    if g == 1:
                        pe.wait_ge(wkv_split, at("nb", 2))
                    if g in (1, 2):
                        project_kv(ps_m[:], 0, g - 1)
                    elif g in (3, 5):
                        project_kv(ps_m[:], 1, (g - 3) // 2)
                    else:
                        pe.wait_ge(vT_copied, at(2, 3 if g == 4 else 4))
                        turn_v(ps_m[:])
                times_v(at, g, 6)

            pe.wait_ge(built, 9)
            with pe.Fori(0, B) as b:
                at0 = counts(pe, b, 0)(0)
                pe.wait_ge(xl_done, b * C + C)
                pe.wait_ge(wkv_split, b * (KV + 1) + 1)
                project_kv(ps_m[:], 0, 0)
                project_kv(ps_o[:], 0, 1)
                pe.wait_ge(rope_swapped, at0(10, 1))
                project_kv(ps_m[:], 1, 0)
                pe.wait_ge(rope_swapped, at0(10, 2))
                project_kv(ps_o[:], 1, 1)
                pe.wait_ge(vT_copied, at0(2, 1))
                turn_v(ps_t[:, 0, :])
                pe.wait_ge(wq_split, b * (KV + 1) + 1)
                project_q(ps_m[:], 0, 0)
                pe.wait_ge(vT_copied, at0(2, 2))
                turn_v(ps_t[:, 1, :])
                project_q(ps_o[:], 0, 1)
                pe.wait_ge(rope_swapped, at0(10, 3))
                project_q(ps_m[:], 1, 0)
                for h in range(H):
                    scores(at0, 0, 0, h, fresh=True)
                pe.wait_ge(v_copied, at0(2, 2))
                pe.wait_ge(rope_swapped, at0(10, 4))
                tiles_of_batch(pe, b, tile)
                atL = counts(pe, b, KV)(0)
                pe.wait_ge(y_added, atL(8, -1))
                times_wo(atL, 0)

                def turn_y(i):
                    pe.wait_ge(f_norm, b * T + i + 1)
                    if i == 0:
                        pe.wait_ge(pT_split, atL(T * TV, CREDIT))
                    if i >= 2:
                        pe.wait_ge(f_lo, b * T + i - 1)
                    for c in range(C):
                        mm = nc.tensor.transpose(ps_t[:, i % 2, c * P:(c + 1) * P], y[:, i, c * P:(c + 1) * P],
                                                 ident[:])
                    mm.then_inc(f_turned, 1)

                def down(i):
                    pe.wait_ge(f_lo, b * T + i + 1)
                    if i == 0:
                        pe.wait_ge(wkv_split, (b + 1) * (KV + 1))
                        pe.wait_ge(y_added, atL(8, 0))
                    if i >= 2:
                        pe.wait_ge(f_copied, b * T + i - 1)
                    bank = (ps_m, ps_o)[i % 2]
                    for c in range(C):
                        mm = three(bank[:, 0:2 * D], x_hi[:, c, i * P:(i + 1) * P], x_lo[:, c, i * P:(i + 1) * P],
                                   wkv_hi[:, c, :], wkv_lo[:, c, :], c == 0, c == C - 1)
                    mm.then_inc(f_h, 1)

                turn_y(0)
                turn_y(1)
                for i in range(T):
                    down(i)
                    if i + 2 < T:
                        turn_y(i + 2)

                def base(i):
                    if i == 0:
                        pe.wait_ge(wq_split, (b + 1) * (KV + 1))
                    if i >= 2:
                        pe.wait_ge(f_sum, b * T + i - 1)
                    for c in range(C):
                        three(ps_s[:, i % 2, 0:E], x_hi[:, c, i * P:(i + 1) * P], x_lo[:, c, i * P:(i + 1) * P],
                              wq_hi[:, c, :], wq_lo[:, c, :], c == 0, False)

                def turn_g(i):
                    pe.wait_ge(f_gated, b * T + i + 1)
                    if i < 2:
                        pe.wait_ge(f_lo, b * T + T)
                    else:
                        pe.wait_ge(f_gT_lo, b * T + i - 1)
                    nc.tensor.transpose(ps_t[:, i % 2, 0:P], gated[:, i % 2, :], ident[:]).then_inc(f_gT, 1)

                def up(i):
                    pe.wait_ge(f_gT_lo, b * T + i + 1)
                    if i == 0:
                        pe.wait_ge(lb_split, b + 1)
                    s = slice((i % 2) * P, (i % 2 + 1) * P)
                    three(ps_s[:, i % 2, 0:E], oT_hi[:, s], oT_lo[:, s], lb_hi[:], lb_lo[:], False, True)\
                        .then_inc(f_out, 1)

                base(0)
                base(1)
                turn_g(0)
                for i in range(T):
                    if i + 1 < T:
                        turn_g(i + 1)
                    up(i)
                    if i + 2 < T:
                        base(i + 2)

        @block.scalar
        def _(act):
            def swap(at, r, bank):
                act.wait_ge(rope_cos, at(10, r + 1))
                if r > 0:
                    act.wait_ge(rope_sum, at(10, r))
                nc.scalar.copy(rope_s[0:D // 2, :], bank[D // 2:D, :]).then_inc(half_swapped, 1)
                nc.scalar.copy(rope_s[D // 2:D, :], bank[0:D // 2, :]).then_inc(rope_swapped, 1)

            def q_high(at, r, pair, half):
                act.wait_ge(rope_sum, at(10, r + 1))
                nc.scalar.copy(q_hi[:, pair % 2, 2 * half:2 * half + 2, :],
                               rope_a[:].rearrange("p (h t) -> p h t", h=2)).then_inc(q_hi_done, 1)

            def k_high(at, r):
                act.wait_ge(rope_sum, at(10, r + 1))
                nc.scalar.copy(k_hi[:, 0:S], k_next[:]).then_inc(k_hi_done, 1)
                nc.scalar.copy(k_hi[:, S:S + P], k_next[:, 0:P]).then_inc(k_hi_done, 1)

            def v_high(half):
                nc.scalar.copy(v_hi[:, 4 * half:4 * half + 4, :], v_next[:, 4 * half:4 * half + 4, :])\
                    .then_inc(v_hi_done, 1)

            def copy_vT(at, dn, half, bank):
                act.wait_ge(v_proj, at(2, 2 * dn + half + 1))
                if dn or half:
                    act.wait_ge(v_turned, at(2, 2 * dn + half))
                nc.scalar.copy(vT[:], bank).then_inc(vT_copied, 1)

            def copy_v(at, dn, half, bank):
                act.wait_ge(v_turned, at(2, 2 * dn + half + 1))
                if dn:
                    act.wait_ge(v_split, at(2, 2 * dn))
                nc.scalar.copy(v_next[:, 4 * half:4 * half + 4, :].rearrange("p k d -> p (k d)"), bank)\
                    .then_inc(v_copied, 1)

            def exp(at, dn, j, h):
                act.wait_ge(negated, at(T * H, dn * T * H + j * H + h + 1))
                nc.scalar.activation(p[:, j % 2, h, :], p[:, j % 2, h, :], ACT.Exp, bias=neg_max[:, j % 2, h:h + 1],
                                     scale=SCALE, accum_out=row_sum[:, j % 2, h:h + 1]).then_inc(exp_done, 1)

            def p_high(at, g, t):
                k = g * TV + t
                act.wait_ge(pT_ready, at(T * TV, k + 1))
                nc.scalar.copy(pT_hi[:, k % 2, :], ps_t[:, k % 2, :]).then_inc(pT_hi_done, 1)

            def tile(g, at, last, first=False):
                dn, j = following(g)
                more = not (last and g == T - 1)
                p_high(at, g, 0)
                p_high(at, g, 1)
                if not last:
                    if g in (2, 3):
                        swap(at, rope_slot(g - 1, "k", last), ps_m)
                    elif g in (4, 6):
                        copy_vT(at, 1, (g - 4) // 2, ps_m[:])
                    elif g in (5, 7):
                        copy_v(at, 1, (g - 5) // 2, ps_m[:])
                for h in range(H):
                    if more:
                        exp(at, dn, j, h)
                    if h < H - 1:
                        p_high(at, g, 2 + h)
                q = not last or g <= 4
                p_high(at, g, 5)
                if g in (0, 7):
                    p_high(at, g, 6)
                if q:
                    r = rope_slot(g, "q", last)
                    swap(at, r, ps_m)
                if g not in (0, 7):
                    p_high(at, g, 6)
                if q:
                    q_high(at, r, ((g + 3) // 2) % 4, (g + 1) % 2)
                if not last:
                    if g == 6:
                        act.wait_ge(s_ready, at(T * H, T * H))
                        k_high(at, rope_slot(2, "k", last))
                    if g == 7:
                        act.wait_ge(v_used, at(1, 1))
                        act.wait_ge(v_copied, at(2, 4))
                        v_high(0)
                act.wait_ge(o_ready, at(8, g + 1))
                nc.scalar.copy(oT_hi[:], ps_o[:]).then_inc(oT_hi_done, 1)
                if not last and g == 7:
                    v_high(1)

            act.wait_ge(built, 9)
            with act.Fori(0, B) as b:
                at0 = counts(act, b, 0)(0)
                for c in range(C):
                    act.wait_ge(xt_in[c], b * 16 + 16)
                    nc.scalar.copy(x_hi[:, c, :], x_raw[:, c * S:(c + 1) * S]).then_inc(xh_done, 1)
                swap(at0, 0, ps_m)
                swap(at0, 1, ps_o)
                copy_vT(at0, 0, 0, ps_m[:])
                k_high(at0, 1)
                copy_v(at0, 0, 0, ps_t[:, 0, :])
                copy_vT(at0, 0, 1, ps_o[:])
                swap(at0, 2, ps_m)
                q_high(at0, 2, 0, 0)
                copy_v(at0, 0, 1, ps_t[:, 1, :])
                swap(at0, 3, ps_o)
                q_high(at0, 3, 0, 1)
                swap(at0, 4, ps_m)
                q_high(at0, 4, 1, 0)
                act.wait_ge(v_copied, at0(2, 2))
                v_high(0)
                v_high(1)
                for h in range(H):
                    exp(at0, 0, 0, h)
                tiles_of_batch(act, b, tile)

                act.wait_ge(f_stat, b * T + T)
                nc.scalar.activation(std[:], mv[:, :, 1], ACT.Sqrt, bias=eps, scale=1.0).then_inc(f_std, 1)

                def h_copy(i):
                    act.wait_ge(f_h, b * T + i + 1)
                    nc.scalar.copy(h_sb[:, i, :], (ps_m, ps_o)[i % 2][:, 0:R + NEXP]).then_inc(f_copied, 1)

                for i in range(T):
                    act.wait_ge(f_turned, b * T + i + 1)
                    nc.scalar.copy(x_hi[:, :, i * P:(i + 1) * P],
                                   ps_t[:, i % 2, :].rearrange("p (c t) -> p c t", c=C)).then_inc(f_hi, 1)
                    if i >= 1:
                        h_copy(i - 1)
                h_copy(T - 1)

                def std_2(i):
                    act.wait_ge(f_stat2, b * T + i + 1)
                    nc.scalar.activation(std2[:, i:i + 1], mv2[:, i, 1:2], ACT.Sqrt, bias=eps, scale=1.0)\
                        .then_inc(f_std2, 1)

                for i in range(T):
                    act.wait_ge(f_gT, b * T + i + 1)
                    if i >= 2:
                        act.wait_ge(f_out, b * T + i - 1)
                    nc.scalar.copy(oT_hi[:, (i % 2) * P:(i % 2 + 1) * P], ps_t[:, i % 2, 0:P]).then_inc(f_gT_hi, 1)
                    if i >= 2:
                        std_2(i - 2)
                std_2(T - 2)
                std_2(T - 1)
                act.wait_ge(f_out, (b + 1) * T)

        @block.vector
        def _(dve):
            def times_cos(at, r, q_before, bank, t0, tokens, heads):
                if r > 0:
                    dve.wait_ge(rope_sum, at(10, r))
                if q_before > 0:
                    dve.wait_ge(q_split, at(8, q_before))
                dve.wait_ge(proj_ready, at(10, r + 1))
                cs = cos_sb[:, t0:t0 + tokens].unsqueeze(1).broadcast_to([P, heads, tokens])
                nc.vector.tensor_tensor(rope_a[:].rearrange("p (h t) -> p h t", h=heads),
                                        bank.rearrange("p (h t) -> p h t", h=heads), cs, ALU.mult)\
                    .then_inc(rope_cos, 1)

            def rotated(at, r, dst):
                dve.wait_ge(rope_cos, at(10, r + 1))
                dve.wait_ge(rope_sin, at(10, r + 1))
                nc.vector.tensor_tensor(dst, rope_a[:], rope_s[:], ALU.add).then_inc(rope_sum, 1)

            def q_low(at, qn, r, pair, half):
                dve.wait_ge(rope_sum, at(10, r + 1))
                dve.wait_ge(q_hi_done, at(8, qn + 1))
                sl = (slice(None), pair % 2, slice(2 * half, 2 * half + 2), slice(None))
                nc.vector.tensor_tensor(q_lo[sl], rope_a[:].rearrange("p (h t) -> p h t", h=2),
                                        q_hi[sl].bitcast(F32), ALU.subtract).then_inc(q_split, 1)

            def k_low(at, dn, r):
                dve.wait_ge(rope_sum, at(10, r + 1))
                dve.wait_ge(k_hi_done, at(2, 2 * dn + 2))
                nc.vector.tensor_tensor(k_lo[:, S:S + P], k_next[:, 0:P], k_hi[:, S:S + P].bitcast(F32),
                                        ALU.subtract)
                nc.vector.tensor_tensor(k_lo[:, 0:S], k_next[:], k_hi[:, 0:S].bitcast(F32), ALU.subtract)\
                    .then_inc(k_split, 1)

            def v_low(at, dn, half):
                dve.wait_ge(v_hi_done, at(2, 2 * dn + half + 1))
                sl = (slice(None), slice(4 * half, 4 * half + 4), slice(None))
                nc.vector.tensor_tensor(v_lo[sl], v_next[sl], v_hi[sl].bitcast(F32), ALU.subtract)\
                    .then_inc(v_split, 1)

            def mask_max(at, dn, j, h):
                start = score_chunks(j, T)[0]
                mask = mask_end[:, 0:KEYS] if j == 0 else mask_end[:, P:KEYS + P] if j == T - 1 else mask_mid[:]
                u = dn * T * H + j * H + h
                wait_apart(dve, s_ready, at(T * H, u + 1))
                nc.vector.tensor_tensor_reduce(p[:, j % 2, h, :], ps_s[:, h % 2, start:start + KEYS], mask, 1.0,
                                               MASKED, ALU.add, ALU.max,
                                               row_max[:, j % 2, h:h + 1]).then_inc(masked, 1)
                dve.wait_ge(masked, at(T * H, u + 1))
                nc.vector.tensor_scalar(neg_max[:, j % 2, h:h + 1], row_max[:, j % 2, h:h + 1], -SCALE, None,
                                        ALU.mult).then_inc(negated, 1)

            def invert(at, dn, j, h):
                dve.wait_ge(exp_done, at(T * H, dn * T * H + j * H + h + 1))
                nc.vector.reciprocal(row_inv[:, j % 2, h:h + 1], row_sum[:, j % 2, h:h + 1]).then_inc(inverted, 1)

            def p_low(at, g, t):
                k = g * TV + t
                dve.wait_ge(pT_hi_done, at(T * TV, k + 1))
                nc.vector.tensor_tensor(pT_lo[:, k % 2, :], ps_t[:, k % 2, :], pT_hi[:, k % 2, :].bitcast(F32),
                                        ALU.subtract).then_inc(pT_split, 1)

            def add_y(at, g):
                i = (g - 1) % T
                dve.wait_ge(wo_ready, at(8, g))
                nc.vector.tensor_tensor(y[:, i, :], ps_m[:], y[:, i, :], ALU.add).then_inc(y_added, 1)

            def tile(g, at, last, first=False):
                dn, j = following(g)
                more = not (last and g == T - 1)
                p_low(at, g, 0)
                p_low(at, g, 1)
                keys = not last and g in (2, 3)
                if keys:
                    rk_ = rope_slot(g - 1, "k", last)
                    times_cos(at, rk_, 3 + g, ps_m[:], (g - 2) * 512, 512, 1)
                if more:
                    mask_max(at, dn, j, 0)
                p_low(at, g, 2)
                if more:
                    mask_max(at, dn, j, 1)
                    invert(at, dn, j, 0)
                if keys:
                    rotated(at, rk_, k_next[:, (g - 2) * 512:(g - 1) * 512])
                if not first:
                    add_y(at, g)
                p_low(at, g, 3)
                if more:
                    mask_max(at, dn, j, 2)
                    invert(at, dn, j, 1)
                p_low(at, g, 4)
                if more:
                    mask_max(at, dn, j, 3)
                    invert(at, dn, j, 2)
                q = not last or g <= 4
                pair, half = ((g + 3) // 2) % 4, (g + 1) % 2
                if q:
                    r = rope_slot(g, "q", last)
                    times_cos(at, r, 3 + g, ps_m[:], pair * 2 * P, 2 * P, 2)
                if more:
                    invert(at, dn, j, 3)
                p_low(at, g, 5)
                p_low(at, g, 6)
                if q:
                    rotated(at, r, rope_a[:])
                    q_low(at, 3 + g, r, pair, half)
                if not last:
                    if g == 6:
                        k_low(at, 1, rope_slot(2, "k", last))
                    if g == 7:
                        v_low(at, 1, 0)
                dve.wait_ge(oT_hi_done, at(8, g + 1))
                nc.vector.tensor_tensor(oT_lo[:], ps_o[:], oT_hi[:].bitcast(F32), ALU.subtract)\
                    .then_inc(oT_split, 1)
                if not last and g == 7:
                    v_low(at, 1, 1)

            LINKS = NEXP + 14

            def feed_forward(b):
                links = [0]

                def step(ins):
                    links[0] += 1
                    ins.then_inc(chain, 1)
                    wait_apart(dve, chain, b * LINKS + links[0])

                for i in range(T):
                    ins = nc.vector.bn_stats(stats[:, i, :], y[:, i, :])
                step(ins)
                for i in range(T):
                    nc.vector.bn_aggr(mv[:, i, :], stats[:, i, :]).then_inc(f_stat, 1)
                dve.wait_ge(f_std, b + 1)
                step(nc.vector.reciprocal(rstd[:], std[:]))

                def normalise(i):
                    nc.vector.tensor_scalar(y[:, i, :], y[:, i, :], mv[:, i, 0:1], rstd[:, i:i + 1], ALU.subtract,
                                            ALU.mult).then_inc(f_norm, 1)

                normalise(0)
                normalise(1)
                for i in range(T):
                    if i + 2 < T:
                        normalise(i + 2)
                    dve.wait_ge(f_hi, b * T + i + 1)
                    s = (slice(None), slice(None), slice(i * P, (i + 1) * P))
                    nc.vector.tensor_tensor(x_lo[s], ps_t[:, i % 2, :].rearrange("p (c t) -> p c t", c=C),
                                            x_hi[s].bitcast(F32), ALU.subtract).then_inc(f_lo, 1)

                def each(v):
                    return v.unsqueeze(1).broadcast_to([P, T, NEXP])

                def per_tile(v):
                    return v.unsqueeze(2).broadcast_to([P, T, NEXP])

                dve.wait_ge(f_copied, b * T + T)
                step(nc.vector.tensor_tensor(z[:], h_sb[:, :, R:R + NEXP], each(br), ALU.add))
                for i in range(T):
                    ins = nc.vector.max(zs[:, i, :], z[:, i, :])
                step(ins)
                step(nc.vector.tensor_copy(zc[:, :, 0:1], zs[:, :, 0:1]))
                for k in range(1, NEXP):
                    step(nc.vector.tensor_tensor(zc[:, :, k:k + 1], zc[:, :, k - 1:k], zs[:, :, k:k + 1], ALU.add))
                step(nc.vector.tensor_tensor(zk[:], zs[:], each(rank), ALU.mult))
                step(nc.vector.tensor_scalar(zk[:], zk[:], 1.0, None, ALU.add))
                step(nc.vector.tensor_tensor(zt[:], zk[:], zc[:], ALU.is_gt))
                step(nc.vector.tensor_reduce(kz, zt[:], AX.X, ALU.add))
                step(nc.vector.tensor_tensor(zt[:], each(rank), per_tile(kz), ALU.is_equal))
                step(nc.vector.tensor_tensor(zt[:], zt[:], zc[:], ALU.mult))
                nc.vector.reciprocal(rk, kz)
                step(nc.vector.tensor_reduce(tau, zt[:], AX.X, ALU.add))
                step(nc.vector.scalar_tensor_tensor(tau, tau, -1.0, rk, ALU.add, ALU.mult))
                step(nc.vector.tensor_tensor(wts[:], z[:], per_tile(tau), ALU.subtract))
                step(nc.vector.tensor_scalar(wts[:], wts[:], 0.0, None, ALU.max))
                assert links[0] == LINKS, links

                def gate(i):
                    if i >= 2:
                        dve.wait_ge(f_gT, b * T + i - 1)
                    nc.vector.tensor_tensor(gated[:, i % 2, :].rearrange("p (e r) -> p e r", e=NEXP),
                                            h_sb[:, i, 0:R].rearrange("p (e r) -> p e r", e=NEXP),
                                            wts[:, i, :].unsqueeze(2).broadcast_to([P, NEXP, RANK]),
                                            ALU.mult).then_inc(f_gated, 1)

                def gated_low(i):
                    dve.wait_ge(f_gT_hi, b * T + i + 1)
                    s = slice((i % 2) * P, (i % 2 + 1) * P)
                    nc.vector.tensor_tensor(oT_lo[:, s], ps_t[:, i % 2, 0:P], oT_hi[:, s].bitcast(F32),
                                            ALU.subtract).then_inc(f_gT_lo, 1)

                def add(i):
                    dve.wait_ge(f_out, b * T + i + 1)
                    dve.wait_ge(f_biased, b * T + i + 1)
                    nc.vector.tensor_tensor(y[:, i, :], ps_s[:, i % 2, 0:E], y[:, i, :], ALU.add)\
                        .then_inc(f_sum, 1)
                    dve.wait_ge(f_sum, b * T + i + 1)
                    nc.vector.bn_stats(stats[:, i, :], y[:, i, :]).then_inc(f_stats, 1)
                    wait_apart(dve, f_stats, b * T + i + 1)
                    nc.vector.bn_aggr(mv2[:, i, :], stats[:, i, :]).then_inc(f_stat2, 1)

                def finish(i):
                    dve.wait_ge(f_std2, b * T + i + 1)
                    nc.vector.reciprocal(rstd2[:, i:i + 1], std2[:, i:i + 1]).then_inc(f_rstd2, 1)
                    dve.wait_ge(f_rstd2, b * T + i + 1)
                    nc.vector.tensor_scalar(y[:, i, :], y[:, i, :], mv2[:, i, 0:1], rstd2[:, i:i + 1],
                                            ALU.subtract, ALU.mult).then_inc(f_done, 1)

                gate(0)
                gate(1)
                gated_low(0)
                for i in range(T):
                    if i + 1 < T:
                        gated_low(i + 1)
                    if i + 2 < T:
                        gate(i + 2)
                    add(i)
                    if i >= 1:
                        finish(i - 1)
                finish(T - 1)

            dve.wait_ge(built, 9)
            dve.sem_inc(pT_split, CREDIT)
            dve.wait_ge(consts_in, 16 * 5)
            with dve.Fori(0, B) as b:
                at0 = counts(dve, b, 0)(0)
                for c in range(C):
                    dve.wait_ge(xh_done, b * C + c + 1)
                    nc.vector.tensor_tensor(x_lo[:, c, :], x_raw[:, c * S:(c + 1) * S], x_hi[:, c, :].bitcast(F32),
                                            ALU.subtract).then_inc(xl_done, 1)
                times_cos(at0, 0, 0, ps_m[:], 0, 512, 1)
                rotated(at0, 0, k_next[:, 0:512])
                times_cos(at0, 1, 0, ps_o[:], 512, 512, 1)
                rotated(at0, 1, k_next[:, 512:1024])
                k_low(at0, 0, 1)
                times_cos(at0, 2, 0, ps_m[:], 0, 2 * P, 2)
                rotated(at0, 2, rope_a[:])
                q_low(at0, 0, 2, 0, 0)
                times_cos(at0, 3, 1, ps_o[:], 0, 2 * P, 2)
                rotated(at0, 3, rope_a[:])
                q_low(at0, 1, 3, 0, 1)
                times_cos(at0, 4, 2, ps_m[:], 2 * P, 2 * P, 2)
                rotated(at0, 4, rope_a[:])
                q_low(at0, 2, 4, 1, 0)
                v_low(at0, 0, 0)
                v_low(at0, 0, 1)
                for h in range(H):
                    mask_max(at0, 0, 0, h)
                    if h:
                        invert(at0, 0, 0, h - 1)
                invert(at0, 0, 0, H - 1)
                dve.wait_ge(y_in, b * 16 + 16)
                tiles_of_batch(dve, b, tile)
                atL = counts(dve, b, KV)(0)
                add_y(atL, 0)
                dve.wait_ge(y_added, atL(8, 0))
                feed_forward(b)


def program(nc, ins, out_shape):
    args = [nc.dram_tensor(f"in_{k}", a.shape, mybir.dt.from_np(a.dtype), kind="ExternalInput").ap()
            for k, a in ins.items()]
    out = nc.dram_tensor("out", out_shape, F32, kind="ExternalOutput").ap()
    attention_ffn(nc, *args, out)


def kernel(**inputs):
    import numpy as np
    import concourse.bacc as bacc
    from concourse.bass_utils import run_bass_kernel_spmd

    a = {k: np.asarray(v) for k, v in inputs.items()}
    x, wq, wk, wv = (a["L0_attn_" + k] for k in ("hidden_states", "Wq", "Wk", "Wv"))
    B, S, E = x.shape
    D, KV = 128, wk.shape[0] // 128
    turned = lambda w: w.reshape(KV, w.shape[0] // KV, E).transpose(0, 2, 1)
    lora_a = a["L0_ffn_lora_A"]
    NEXP, _, RANK = lora_a.shape
    down = np.zeros((1, E, 2 * D), np.float32)
    down[0, :, 0:NEXP * RANK] = lora_a.transpose(1, 0, 2).reshape(E, NEXP * RANK)
    down[0, :, NEXP * RANK:NEXP * RANK + NEXP] = a["L0_ffn_W_router"].T
    exponent = (np.arange(0, D, 2, dtype=np.float32) / np.float32(D)).astype(np.float32)
    power = np.power(10000.0, exponent.astype(np.float64)).astype(np.float32)
    inverse = (np.float32(1.0) / power).astype(np.float32)
    angle = (np.arange(S, dtype=np.float32)[None, :] * inverse[:, None]).astype(np.float64)
    cos, sin = np.cos(angle).astype(np.float32), np.sin(angle).astype(np.float32)
    ins = {
        "xT": x.transpose(0, 2, 1),
        "x": x,
        "wqT": np.concatenate([turned(wq), a["L0_ffn_W_base"].T[None]], 0),
        "wkvT": np.concatenate([np.concatenate([turned(wk), turned(wv)], 2), down], 0),
        "woT": a["L0_attn_Wo"].T.reshape(KV, 4 * D, E),
        "loraB": a["L0_ffn_lora_B"].reshape(NEXP * RANK, E),
        "b_base": a["L0_ffn_b_base"],
        "b_router": a["L0_ffn_b_router"],
        "cosT": np.concatenate([cos, cos], 0),
        "sinT": np.concatenate([-sin, sin], 0),
        "ranks": np.arange(1, NEXP + 1, dtype=np.float32),
    }
    ins = {k: np.ascontiguousarray(v) for k, v in ins.items()}
    nc = bacc.Bacc("TRN2", target_bir_lowering=False, num_devices=1)
    program(nc, ins, x.shape)
    r = run_bass_kernel_spmd(nc, [{f"in_{k}": v for k, v in ins.items()}], core_ids=[0])
    return r.results[0]["out"]
```

```python
from contextlib import ExitStack

import concourse.bass as bass
from concourse import mybir
from concourse.alu_op_type import AluOpType as ALU

ACT = mybir.ActivationFunctionType
AX = mybir.AxisListType
F32 = mybir.dt.float32
F32R = mybir.dt.float32r
BF16 = mybir.dt.bfloat16

P = 128
HEADS_PER_KV = 4
EPS = 1e-5
MASKED = -3.0e38


def score_chunks(i, tiles):
    first_bank = 3 if i in (2, 4) else 4
    start = (4 - first_bank) * P
    cuts = {0: [4, 3], 1: [4, 3], 2: [3, 2, 2], 3: [4, 3], 4: [3, 4], 5: [2, 2, 3], 6: [2, 2, 3], 7: [4, 3]}[i]
    chunks, t = [], 0
    for n in cuts:
        block = (i + 1 + t) % tiles
        assert block + n <= tiles + 1
        chunks.append((start + t * P, block, n))
        t += n
    assert t == tiles - 1
    return start, chunks


def attention_ffn(nc, xT, x, wqT, wkvT, woT, loraB, b_base, b_router, cosT, sinT, ranks, out):
    B, S, E = x.shape
    KV = woT.shape[0]
    H = HEADS_PER_KV
    D = wkvT.shape[2] // 2
    C = E // P
    T = S // P
    TV = T - 1
    KEYS = TV * P
    R = loraB.shape[0]
    NEXP = b_router.shape[0]
    RANK = R // NEXP
    HP = H * P
    SCALE = float(D) ** -0.5
    assert D == P and R == P and T == 8 and C == 4 and H == 4 and E == 512

    ctx = ExitStack()
    with ctx:
        def sb(name, shape, dt=F32):
            return ctx.enter_context(nc.sbuf_tensor(name, shape, dt))

        def sem(name):
            return ctx.enter_context(nc.semaphore(name))

        x_hi = sb("x_hi", [P, C, S], F32R)
        x_lo = sb("x_lo", [P, C, S], F32R)
        y = sb("y", [P, T, E])
        k_hi = sb("k_hi", [P, (T + 1) * P], F32R)
        k_lo = sb("k_lo", [P, (T + 1) * P], F32R)
        k_next = sb("k_next", [P, S])
        v_hi = sb("v_hi", [P, T, D], F32R)
        v_lo = sb("v_lo", [P, T, D], F32R)
        v_next = sb("v_next", [P, T, D])
        vT = sb("vT", [P, 4 * P])
        q_hi = sb("q_hi", [P, 2, H, 2 * P], F32R)
        q_lo = sb("q_lo", [P, 2, H, 2 * P], F32R)
        p = sb("p", [P, 2, H, KEYS])
        pT_hi = sb("pT_hi", [P, 2, HP], F32R)
        pT_lo = sb("pT_lo", [P, 2, HP], F32R)
        oT_hi = sb("oT_hi", [P, HP], F32R)
        oT_lo = sb("oT_lo", [P, HP], F32R)
        wq_hi = sb("wq_hi", [P, C, HP], F32R)
        wq_lo = sb("wq_lo", [P, C, HP], F32R)
        wkv_hi = sb("wkv_hi", [P, C, 2 * D], F32R)
        wkv_lo = sb("wkv_lo", [P, C, 2 * D], F32R)
        wo_hi = sb("wo_hi", [P, H, E], F32R)
        wo_lo = sb("wo_lo", [P, H, E], F32R)
        lb_hi = sb("lb_hi", [P, E], F32R)
        lb_lo = sb("lb_lo", [P, E], F32R)
        stage = [sb(f"stage{i}", [P, 2 * HP]) for i in range(2)]
        rope_a = sb("rope_a", [P, 2 * 2 * P])
        rope_s = sb("rope_s", [P, 2 * 2 * P])
        cos_sb = sb("cos_sb", [P, S])
        sin_sb = sb("sin_sb", [P, S])
        mask_mid = sb("mask_mid", [P, KEYS], BF16)
        mask_end = sb("mask_end", [P, KEYS + P], BF16)
        ident = sb("ident", [P, P])
        row_max = sb("row_max", [P, 2, H])
        neg_max = sb("neg_max", [P, 2, H])
        row_sum = sb("row_sum", [P, 2, H])
        row_inv = sb("row_inv", [P, 2, H])
        h_sb = sb("h_sb", [P, T, R + NEXP])
        bb = sb("bb", [P, E])
        small = sb("small", [P, 3 * T + 2 * NEXP + 4])
        stats = sb("stats", [P, T, 6])
        mv = sb("mv", [P, T, 2])
        std = sb("std", [P, T])
        rstd = sb("rstd", [P, T])
        mv2 = sb("mv2", [P, T, 2])
        std2 = sb("std2", [P, T])
        rstd2 = sb("rstd2", [P, T])
        z = sb("z", [P, T, NEXP])
        zs = sb("zs", [P, T, NEXP])
        zc = sb("zc", [P, T, NEXP])
        zk = sb("zk", [P, T, NEXP])
        zt = sb("zt", [P, T, NEXP])
        wts = sb("wts", [P, T, NEXP])
        kz, tau, rk = (small[:, i * T:(i + 1) * T] for i in range(3))
        br = small[:, 3 * T:3 * T + NEXP]
        rank = small[:, 3 * T + NEXP:3 * T + 2 * NEXP]
        eps = small[:, 3 * T + 2 * NEXP:3 * T + 2 * NEXP + 1]

        ps_s = ctx.enter_context(nc.psum_tensor("ps_s", [P, 2, 1024], F32))
        ps_t = ctx.enter_context(nc.psum_tensor("ps_t", [P, 2, 512], F32))
        ps_o = ctx.enter_context(nc.psum_tensor("ps_o", [P, 512], F32))
        ps_m = ctx.enter_context(nc.psum_tensor("ps_m", [P, 512], F32))

        p_flat = p[:, :, :, :].rearrange("p a h k -> p (a h k)")
        x_raw = p_flat[:, 0:C * S]
        first_q = [p_flat[:, C * S + i * 4 * P:C * S + (i + 1) * 4 * P] for i in range(6)]
        assert C * S + 6 * 4 * P <= 2 * H * KEYS
        first_rope = [(k_next[:, 0:512], rope_s[:]), (k_next[:, 512:1024], rope_a[:])] \
            + [(first_q[2 * i], first_q[2 * i + 1]) for i in range(3)]

        consts_in = sem("consts_in")
        waits_passed = sem("waits_passed")
        opened = sem("opened")
        built = sem("built")
        xt_in = [sem(f"xt_in{c}") for c in range(C)]
        y_in = sem("y_in")
        stage_in = [sem("stage_in0"), sem("stage_in1")]
        stage1_free = sem("stage1_free")
        wkv_split, wq_split, wo_split = sem("wkv_split"), sem("wq_split"), sem("wo_split")
        lb_split = sem("lb_split")
        w_hi_done = sem("w_hi_done")
        xh_done = sem("xh_done")
        x0_done = sem("x0_done")
        xl_done = sem("xl_done")
        proj_ready = sem("proj_ready")
        half_swapped = sem("half_swapped")
        rope_cos, rope_swapped = sem("rope_cos"), sem("rope_swapped")
        rope_sin, rope_sum = sem("rope_sin"), sem("rope_sum")
        q_hi_done, q_split = sem("q_hi_done"), sem("q_split")
        k_hi_done, k_split = sem("k_hi_done"), sem("k_split")
        v_proj, vT_copied, v_turned, v_copied = sem("v_proj"), sem("vT_copied"), sem("v_turned"), sem("v_copied")
        v_used = sem("v_used")
        v_hi_done, v_split = sem("v_hi_done"), sem("v_split")
        s_ready = sem("s_ready")
        masked = sem("masked")
        negated = sem("negated")
        exp_done = sem("exp_done")
        inverted = sem("inverted")
        normed = sem("normed")
        pT_ready = sem("pT_ready")
        pT_hi_done, pT_split = sem("pT_hi_done"), sem("pT_split")
        o_ready = sem("o_ready")
        oT_hi_done, oT_split = sem("oT_hi_done"), sem("oT_split")
        wo_ready = sem("wo_ready")
        y_added = sem("y_added")
        chain = sem("chain")
        f_stat1 = sem("f_stat1")
        f_mean2 = sem("f_mean2")
        f_stat, f_std, f_rstd, f_norm = sem("f_stat"), sem("f_std"), sem("f_rstd"), sem("f_norm")
        f_turned, f_hi, f_lo, f_h, f_copied = (sem("f_turned"), sem("f_hi"), sem("f_lo"), sem("f_h"), sem("f_copied"))
        f_stats = sem("f_stats")
        f_biased = sem("f_biased")
        f_gated, f_gT, f_gT_hi, f_gT_lo = sem("f_gated"), sem("f_gT"), sem("f_gT_hi"), sem("f_gT_lo")
        f_out, f_sum, f_stat2 = sem("f_out"), sem("f_sum"), sem("f_stat2")
        f_std2, f_rstd2, f_done = sem("f_std2"), sem("f_rstd2"), sem("f_done")
        stored = sem("stored")

        def rope_slot(g, what, last):
            order = []
            for gg in range(T):
                if not last or gg <= 4:
                    order.append((gg, "q"))
                if not last and gg in (1, 2):
                    order.append((gg, "k"))
            return 5 + order.index((g, what))

        def ffn_bank(i):
            return ps_s[:, i % 2, i // 2 % 2 * E:(i // 2 % 2 + 1) * E]

        K_CUT = 5 * P
        CREDIT = 2
        gated = vT[:, 0:2 * P].rearrange("p (a n) -> p a n", a=2)

        block = ctx.enter_context(nc.Block())

        def counts(eng, b, kv):
            n = b * KV + kv
            held = {k: eng.snap(n * k) for k in (1, 2, 5, 8, 10, T * H, T * TV)}
            held["nb"] = eng.snap(n + b)

            def after(dn):
                def at(k, c):
                    return held[k] + ((dn if k == "nb" else dn * k) + c)
                return at
            return after

        def wait_apart(eng, s, count):
            eng.wait_ge(s, count)
            eng.sem_inc(waits_passed, 1)

        def tiles_of_batch(eng, b, tile):
            after = counts(eng, b, 0)
            tile(0, after(0), last=False, first=True)
            with eng.Fori(0, KV - 1) as kv:
                after = counts(eng, b, kv)
                for g in range(1, T):
                    tile(g, after(0), last=False)
                tile(0, after(1), last=False)
            after = counts(eng, b, KV - 1)
            for g in range(1, T):
                tile(g, after(0), last=True)

        def following(g):
            return (1, 0) if g == T - 1 else (0, g + 1)

        @block.sync
        def _(sp):
            sp.dma_start(cos_sb[:], cosT).then_inc(consts_in, 16)
            sp.dma_start(sin_sb[:], sinT).then_inc(consts_in, 16)
            sp.dma_start(rank, ranks.rearrange("(a n) -> a n", a=1).broadcast_to([P, NEXP])).then_inc(consts_in, 16)
            sp.dma_start(br, b_router.rearrange("(a n) -> a n", a=1).broadcast_to([P, NEXP])).then_inc(consts_in, 16)
            sp.dma_start(bb[:], b_base.rearrange("(a n) -> a n", a=1).broadcast_to([P, E])).then_inc(consts_in, 16)

            def load(i, src):
                sp.dma_start(stage[i][:].rearrange("p (c n) -> p c n", c=src.shape[1]), src).then_inc(stage_in[i], 16)

            def of_group(w, kv):
                return w[bass.ds(kv, 1)].rearrange("a (c p) n -> p (a c) n", p=P)

            sp.sem_inc(stored, 1)
            with sp.Fori(0, B) as b:
                sp.wait_ge(opened, b + 1)
                load(0, of_group(wkvT, 0))
                for c in range(C):
                    sp.dma_start(x_raw[:, c * S:(c + 1) * S],
                                 xT[bass.ds(b, 1), c * P:(c + 1) * P, :].rearrange("a p s -> (a p) s"))\
                        .then_inc(xt_in[c], 16)
                load(1, of_group(wqT, 0)[:, 0:2])
                sp.wait_ge(wkv_split, b * (KV + 1) + 1)
                load(0, of_group(wqT, 0)[:, 2:4])
                sp.wait_ge(stored, b * (16 * T) + 1)
                sp.dma_start(y[:], x[bass.ds(b, 1)].rearrange("a (t p) e -> p (a t) e", p=P)).then_inc(y_in, 16)
                sp.wait_ge(wq_split, b * (KV + 1) + 1)
                load(0, of_group(wkvT, 1))

                def weights_of_group(kv, last):
                    nb, n2b = b * (KV + 1) + kv, b * (2 * KV + 1) + kv * 2
                    sp.wait_ge(stage1_free, n2b + 1)
                    load(1, of_group(woT, kv)[:, 0:2])
                    sp.wait_ge(wkv_split, nb + 2)
                    load(0, of_group(woT, kv)[:, 2:4])
                    sp.wait_ge(stage1_free, n2b + 2)
                    load(1, of_group(wqT, kv + 1)[:, 0:2])
                    sp.wait_ge(wo_split, b * KV + kv + 1)
                    load(0, of_group(wqT, kv + 1)[:, 2:4])
                    if not last:
                        sp.wait_ge(wq_split, nb + 2)
                        load(0, of_group(wkvT, kv + 2))

                with sp.Fori(0, KV - 1) as kv:
                    weights_of_group(kv, False)
                weights_of_group(KV - 1, True)
                sp.wait_ge(stage1_free, (b + 1) * (2 * KV + 1))
                sp.dma_start(stage[1][:, 0:E], loraB).then_inc(stage_in[1], 16)
            sp.wait_ge(stored, B * 16 * T + 1)

        @block.gpsimd
        def _(pool):
            nc.gpsimd.memset(ident[:], 0.0).then_inc(built, 1)
            nc.gpsimd.memset(mask_mid[:], 0.0).then_inc(built, 1)
            nc.gpsimd.memset(mask_end[:], 0.0).then_inc(built, 1)
            nc.gpsimd.memset(eps, EPS).then_inc(built, 1)
            pool.wait_ge(built, 4)
            nc.gpsimd.affine_select(out=ident[:], in_=ident[:], compare_op=ALU.not_equal, fill=1.0, base=0,
                                    pattern=[[-1, P]], channel_multiplier=1).then_inc(built, 1)
            for m, end in ((mask_mid, KEYS), (mask_end, KEYS + P)):
                nc.gpsimd.affine_select(out=m[:, 0:P], in_=m[:, 0:P], compare_op=ALU.is_ge, fill=MASKED, base=0,
                                        pattern=[[1, P]], channel_multiplier=-1).then_inc(built, 1)
                nc.gpsimd.affine_select(out=m[:, end - P:end], in_=m[:, end - P:end], compare_op=ALU.is_ge,
                                        fill=MASKED, base=0, pattern=[[-1, P]],
                                        channel_multiplier=1).then_inc(built, 1)

            def split(i, loaded, hi, lo, width, hi_count):
                wait_apart(pool, stage_in[i], loaded)
                src = stage[i][:, 0:width]
                nc.gpsimd.tensor_scalar(hi, src, 1.0, 1.0, ALU.mult, ALU.mult).then_inc(w_hi_done, 1)
                pool.wait_ge(w_hi_done, hi_count)
                return nc.gpsimd.tensor_tensor(lo, src, hi.bitcast(F32), ALU.subtract)

            def chunks(t, a=0, z_=C):
                return t[:, a:z_].rearrange("p c n -> p (c n)")

            def norm(at, dn, j, h):
                wait_apart(pool, inverted, at(T * H, dn * T * H + j * H + h + 1))
                nc.gpsimd.tensor_scalar(p[:, j % 2, h, :], p[:, j % 2, h, :], row_inv[:, j % 2, h:h + 1], 1.0,
                                        ALU.mult, ALU.mult).then_inc(normed, 1)

            def times_sin(at, r, t0, tokens, heads, swapped=rope_s[:]):
                pool.wait_ge(rope_swapped, at(10, r + 1))
                s = swapped.rearrange("p (h t) -> p h t", h=heads)
                sn = sin_sb[:, t0:t0 + tokens].unsqueeze(1).broadcast_to([P, heads, tokens])
                nc.gpsimd.tensor_tensor(s, s, sn, ALU.mult).then_inc(rope_sin, 1)

            pool.sem_inc(opened, 1)
            with pool.Fori(0, B) as b:
                hi0 = pool.snap(b * (5 * KV + 4))
                in0, in1 = pool.snap(b * (16 * (3 * KV + 2))), pool.snap(b * (16 * (2 * KV + 2)))
                split(0, in0 + 16, chunks(wkv_hi), chunks(wkv_lo), 2 * HP, hi0 + 1).then_inc(wkv_split, 1)
                split(1, in1 + 16, chunks(wq_hi, 0, 2), chunks(wq_lo, 0, 2), 2 * HP, hi0 + 2)\
                    .then_inc(stage1_free, 1)
                split(0, in0 + 32, chunks(wq_hi, 2, 4), chunks(wq_lo, 2, 4), 2 * HP, hi0 + 3)\
                    .then_inc(wq_split, 1)
                pool.wait_ge(consts_in, 16 * 5)
                at0 = counts(pool, b, 0)(0)
                times_sin(at0, 0, 0, 512, 1, first_rope[0][1])
                times_sin(at0, 1, 512, 512, 1, first_rope[1][1])
                times_sin(at0, 2, 0, 2 * P, 2, first_rope[2][1])
                times_sin(at0, 3, 0, 2 * P, 2, first_rope[3][1])
                for h in range(H):
                    norm(at0, 0, 0, h)
                times_sin(at0, 4, 2 * P, 2 * P, 2, first_rope[4][1])
                pool.wait_ge(v_proj, at0(2, 2))
                split(0, in0 + 16 * 3, chunks(wkv_hi), chunks(wkv_lo), 2 * HP, hi0 + 4).then_inc(wkv_split, 1)

                b4, b2_16 = pool.snap(b * 4), pool.snap(b * 32)

                def tile(g, at, last, first=False):
                    dn, j = following(g)
                    more = not (last and g == T - 1)
                    if not last and g in (2, 3):
                        times_sin(at, rope_slot(g - 1, "k", last), (g - 2) * 512, 512, 1)
                    if more:
                        norm(at, dn, j, 0)
                    if g == 0:
                        if not first:
                            pool.wait_ge(wo_ready, at(8, 0))
                        split(1, at(2, 2) * 16 + b2_16, chunks(wo_hi, 0, 2), chunks(wo_lo, 0, 2), 2 * HP,
                              at(5, 5) + b4).then_inc(stage1_free, 1)
                    if more:
                        for h in range(1, H):
                            norm(at, dn, j, h)
                    if not last or g <= 4:
                        times_sin(at, rope_slot(g, "q", last), ((g + 3) // 2) % 4 * 2 * P, 2 * P, 2)
                    if g == 0:
                        split(0, at(2, 4) * 16 + at(1, 0) * 16 + b2_16, chunks(wo_hi, 2, 4), chunks(wo_lo, 2, 4),
                              2 * HP, at(5, 6) + b4).then_inc(wo_split, 1)
                    if g == 4:
                        pool.wait_ge(proj_ready, at(10, rope_slot(4, "q", last) + 1))
                        split(1, at(2, 3) * 16 + b2_16, chunks(wq_hi, 0, 2), chunks(wq_lo, 0, 2), 2 * HP,
                              at(5, 7) + b4).then_inc(stage1_free, 1)
                        split(0, at(2, 5) * 16 + at(1, 0) * 16 + b2_16, chunks(wq_hi, 2, 4), chunks(wq_lo, 2, 4),
                              2 * HP, at(5, 8) + b4).then_inc(wq_split, 1)
                    if g == 6 and not last:
                        pool.wait_ge(v_proj, at(2, 4))
                        split(0, at(2, 6) * 16 + at(1, 0) * 16 + b2_16, chunks(wkv_hi), chunks(wkv_lo), 2 * HP,
                              at(5, 9) + b4).then_inc(wkv_split, 1)
                tiles_of_batch(pool, b, tile)
                split(1, (b + 1) * (16 * (2 * KV + 2)), lb_hi[:], lb_lo[:], E, (b + 1) * (5 * KV + 4))\
                    .then_inc(lb_split, 1)
                for i in range(T):
                    pool.wait_ge(f_turned, b * T + i + 1)
                    nc.gpsimd.tensor_tensor(y[:, i, :], y[:, i, :], bb[:], ALU.add).then_inc(f_biased, 1)
                pool.wait_ge(lb_split, b + 1)
                pool.sem_inc(opened, 1)
                pool.wait_ge(f_out, (b + 1) * T - 2)

        @block.tensor
        def _(pe):
            def three(out_, a_hi, a_lo, b_hi, b_lo, first, last):
                nc.tensor.matmul(out_, a_hi, b_hi, start=first, stop=False)
                nc.tensor.matmul(out_, a_hi, b_lo, start=False, stop=False)
                return nc.tensor.matmul(out_, a_lo, b_hi, start=False, stop=last)

            def project_q(bank, pair, half):
                t0 = pair * 2 * P
                for hh in range(2):
                    h = 2 * half + hh
                    for c in range(C):
                        mm = three(bank[:, hh * 2 * P:(hh + 1) * 2 * P], wq_hi[:, c, h * P:(h + 1) * P],
                                   wq_lo[:, c, h * P:(h + 1) * P], x_hi[:, c, t0:t0 + 2 * P],
                                   x_lo[:, c, t0:t0 + 2 * P], c == 0, c == C - 1)
                mm.then_inc(proj_ready, 1)

            def project_kv(bank, which, half):
                w, t0 = which * D, half * 512
                for c in range(C):
                    mm = three(bank, wkv_hi[:, c, w:w + D], wkv_lo[:, c, w:w + D], x_hi[:, c, t0:t0 + 512],
                               x_lo[:, c, t0:t0 + 512], c == 0, c == C - 1)
                mm.then_inc(v_proj if which else proj_ready, 1)

            def turn_v(bank):
                for k in range(4):
                    mm = nc.tensor.transpose(bank[:, k * P:(k + 1) * P], vT[:, k * P:(k + 1) * P], ident[:])
                mm.then_inc(v_turned, 1)

            def scores(at, dn, j, h, fresh=False):
                if j % 2 == 0 and h % 2 == 0:
                    pe.wait_ge(q_split, at(8, dn * 8 + j + h // 2 + 1))
                if not (fresh and h < 2):
                    pe.wait_ge(masked, at(T * H, dn * T * H + j * H + h - 1))
                slot, off = h % 2, (j % 2) * P
                for part, (col, kb, cnt) in enumerate(score_chunks(j, T)[1]):
                    if h == 0 and j == 0:
                        pe.wait_ge(k_split, at(2, 2 * dn + part + 1))
                    mm = three(ps_s[:, slot, col:col + cnt * P],
                               q_hi[:, (j // 2) % 2, h, off:off + P], q_lo[:, (j // 2) % 2, h, off:off + P],
                               k_hi[:, kb * P:(kb + cnt) * P], k_lo[:, kb * P:(kb + cnt) * P], True, True)
                mm.then_inc(s_ready, 1)

            def turn_p(at, g, t):
                if t == 0:
                    pe.wait_ge(normed, at(T * H, (g + 1) * H))
                k = g * TV + t
                pe.wait_ge(pT_split, at(T * TV, k - 1 + CREDIT))
                for h in range(H):
                    mm = nc.tensor.transpose(ps_t[:, k % 2, h * P:(h + 1) * P], p[:, g % 2, h, t * P:(t + 1) * P],
                                             ident[:])
                mm.then_inc(pT_ready, 1)

            def times_v(at, g, t, first=False):
                k, j = g * TV + t, (g + 1 + t) % T
                if t == 0 and not first:
                    pe.wait_ge(oT_split, at(8, g))
                if g == 0 and t in (0, 3):
                    pe.wait_ge(v_split, at(2, 1 if t == 0 else 2))
                pe.wait_ge(pT_hi_done, at(T * TV, k + 1))
                nc.tensor.matmul(ps_o[:], v_hi[:, j, :], pT_hi[:, k % 2, :], start=t == 0, stop=False)
                nc.tensor.matmul(ps_o[:], v_lo[:, j, :], pT_hi[:, k % 2, :], start=False, stop=False)
                pe.wait_ge(pT_split, at(T * TV, k + 1 + CREDIT))
                mm = nc.tensor.matmul(ps_o[:], v_hi[:, j, :], pT_lo[:, k % 2, :], start=False, stop=t == TV - 1)
                if t == TV - 1:
                    mm.then_inc(o_ready, 1)
                elif g == T - 1 and t == 3:
                    mm.then_inc(v_used, 1)

            def times_wo(at, g):
                pe.wait_ge(oT_hi_done, at(8, g))
                if g == 1:
                    pe.wait_ge(wo_split, at(1, 1))
                for h in range(H):
                    s = slice(h * P, (h + 1) * P)
                    nc.tensor.matmul(ps_m[:], oT_hi[:, s], wo_hi[:, h, :], start=h == 0, stop=False)
                    nc.tensor.matmul(ps_m[:], oT_hi[:, s], wo_lo[:, h, :], start=False, stop=False)
                pe.wait_ge(oT_split, at(8, g))
                for h in range(H):
                    s = slice(h * P, (h + 1) * P)
                    mm = nc.tensor.matmul(ps_m[:], oT_lo[:, s], wo_hi[:, h, :], start=False, stop=h == H - 1)
                mm.then_inc(wo_ready, 1)

            def projections_read(at, g, last):
                if g == 0:
                    pe.wait_ge(rope_swapped, at(10, 5))
                elif last and g >= 6:
                    pe.wait_ge(y_added, at(8, g - 1))
                elif not last and g in (2, 3):
                    pe.wait_ge(rope_swapped, at(10, rope_slot(g - 1, "k", last) + 1))
                elif not last and g in (4, 6):
                    pe.wait_ge(vT_copied, at(2, 3 if g == 4 else 4))
                elif not last and g in (5, 7):
                    pe.wait_ge(v_copied, at(2, 3 if g == 5 else 4))
                else:
                    pe.wait_ge(rope_swapped, at(10, rope_slot(g - 1, "q", last) + 1))

            def tile(g, at, last, first=False):
                dn, j = following(g)
                more = not (last and g == T - 1)
                turn_p(at, g, 0)
                if not first:
                    times_v(at, g - 1, TV - 1)
                turn_p(at, g, 1)
                if more:
                    scores(at, dn, j, 0)
                    scores(at, dn, j, 1)
                times_v(at, g, 0, first)
                turn_p(at, g, 2)
                projections_read(at, g, last)
                if not first:
                    times_wo(at, g)
                if more:
                    scores(at, dn, j, 2)
                times_v(at, g, 1)
                turn_p(at, g, 3)
                times_v(at, g, 2)
                turn_p(at, g, 4)
                if more:
                    scores(at, dn, j, 3)
                if not last or g <= 4:
                    if g == 5:
                        pe.wait_ge(wq_split, at("nb", 2))
                    if not first:
                        pe.wait_ge(y_added, at(8, g))
                    project_q(ps_m[:], ((g + 3) // 2) % 4, (g + 1) % 2)
                times_v(at, g, 3)
                turn_p(at, g, 5)
                times_v(at, g, 4)
                turn_p(at, g, 6)
                times_v(at, g, 5)
                if not last and 1 <= g <= 6:
                    pe.wait_ge(rope_swapped, at(10, rope_slot(g, "q", last) + 1))
                    if g == 1:
                        pe.wait_ge(wkv_split, at("nb", 2))
                    if g in (1, 2):
                        project_kv(ps_m[:], 0, g - 1)
                    elif g in (3, 5):
                        project_kv(ps_m[:], 1, (g - 3) // 2)
                    else:
                        pe.wait_ge(vT_copied, at(2, 3 if g == 4 else 4))
                        turn_v(ps_m[:])
            pe.wait_ge(built, 9)
            with pe.Fori(0, B) as b:
                at0 = counts(pe, b, 0)(0)
                pe.wait_ge(wkv_split, b * (KV + 1) + 1)
                for c in range(C):
                    pe.wait_ge(xl_done, b * C + c + 1)
                    for i, bank in enumerate((ps_m[:], ps_o[:])):
                        mm = three(bank, wkv_hi[:, c, 0:D], wkv_lo[:, c, 0:D], x_hi[:, c, i * 512:(i + 1) * 512],
                                   x_lo[:, c, i * 512:(i + 1) * 512], c == 0, c == C - 1)
                        if c == C - 1:
                            mm.then_inc(proj_ready, 1)
                pe.wait_ge(wq_split, b * (KV + 1) + 1)
                project_q(ps_t[:, 0, :], 0, 0)
                project_q(ps_t[:, 1, :], 0, 1)
                pe.wait_ge(rope_swapped, at0(10, 1))
                project_kv(ps_m[:], 1, 0)
                for h in range(H):
                    scores(at0, 0, 0, h, fresh=True)
                pe.wait_ge(rope_swapped, at0(10, 2))
                project_kv(ps_o[:], 1, 1)
                pe.wait_ge(vT_copied, at0(2, 1))
                pe.wait_ge(rope_swapped, at0(10, 3))
                turn_v(ps_t[:, 0, :])
                project_q(ps_m[:], 1, 0)
                pe.wait_ge(vT_copied, at0(2, 2))
                turn_v(ps_o[:])
                pe.wait_ge(rope_swapped, at0(10, 4))
                pe.wait_ge(v_copied, at0(2, 1))
                tiles_of_batch(pe, b, tile)
                atL = counts(pe, b, KV)(0)
                times_v(atL, -1, TV - 1)
                pe.wait_ge(y_added, atL(8, -1))
                times_wo(atL, 0)

                def turn_y(i):
                    pe.wait_ge(f_norm, b * T + i + 1)
                    if i == 0:
                        pe.wait_ge(pT_split, atL(T * TV, CREDIT))
                    if i >= 2:
                        pe.wait_ge(f_lo, b * T + i - 1)
                    for c in range(C):
                        mm = nc.tensor.transpose(ps_t[:, i % 2, c * P:(c + 1) * P], y[:, i, c * P:(c + 1) * P],
                                                 ident[:])
                    mm.then_inc(f_turned, 1)

                def down(i):
                    pe.wait_ge(f_lo, b * T + i + 1)
                    if i == 0:
                        pe.wait_ge(wkv_split, (b + 1) * (KV + 1))
                    if i == 1:
                        pe.wait_ge(y_added, atL(8, 0))
                    if i >= 2:
                        pe.wait_ge(f_copied, b * T + i - 1)
                    bank = (ps_o, ps_m)[i % 2]
                    for c in range(C):
                        mm = three(bank[:, 0:2 * D], x_hi[:, c, i * P:(i + 1) * P], x_lo[:, c, i * P:(i + 1) * P],
                                   wkv_hi[:, c, :], wkv_lo[:, c, :], c == 0, c == C - 1)
                    mm.then_inc(f_h, 1)

                turn_y(0)
                turn_y(1)
                for i in range(T):
                    down(i)
                    if i + 2 < T:
                        turn_y(i + 2)

                def base(i):
                    if i == 0:
                        pe.wait_ge(wq_split, (b + 1) * (KV + 1))
                    if i >= 4:
                        pe.wait_ge(f_sum, b * T + i - 3)
                    for c in range(C):
                        three(ffn_bank(i), x_hi[:, c, i * P:(i + 1) * P], x_lo[:, c, i * P:(i + 1) * P],
                              wq_hi[:, c, :], wq_lo[:, c, :], c == 0, False)

                def turn_g(i):
                    pe.wait_ge(f_gated, b * T + i + 1)
                    if i < 2:
                        pe.wait_ge(f_lo, b * T + T)
                    else:
                        pe.wait_ge(f_gT_lo, b * T + i - 1)
                    nc.tensor.transpose(ps_t[:, i % 2, 0:P], gated[:, i % 2, :], ident[:]).then_inc(f_gT, 1)

                def up(i):
                    pe.wait_ge(f_gT_lo, b * T + i + 1)
                    if i == 0:
                        pe.wait_ge(lb_split, b + 1)
                    s = slice((i % 2) * P, (i % 2 + 1) * P)
                    three(ffn_bank(i), oT_hi[:, s], oT_lo[:, s], lb_hi[:], lb_lo[:], False, True)\
                        .then_inc(f_out, 1)

                for i in range(4):
                    base(i)
                turn_g(0)
                for i in range(T):
                    if i + 1 < T:
                        turn_g(i + 1)
                    up(i)
                    if i >= 1 and i + 3 < T:
                        base(i + 3)

        @block.scalar
        def _(act):
            def swap(at, r, bank):
                act.wait_ge(rope_cos, at(10, r + 1))
                dst = first_rope[r][1] if r < 5 else rope_s[:]
                if r >= 5:
                    act.wait_ge(rope_sum, at(10, r))
                nc.scalar.copy(dst[0:D // 2, :], bank[D // 2:D, :]).then_inc(half_swapped, 1)
                nc.scalar.copy(dst[D // 2:D, :], bank[0:D // 2, :]).then_inc(rope_swapped, 1)

            def q_high(at, r, pair, half):
                act.wait_ge(rope_sum, at(10, r + 1))
                src = first_rope[r][0] if r < 5 else rope_a[:]
                nc.scalar.copy(q_hi[:, pair % 2, 2 * half:2 * half + 2, :],
                               src.rearrange("p (h t) -> p h t", h=2)).then_inc(q_hi_done, 1)

            def k_high(at, r, part):
                act.wait_ge(rope_sum, at(10, r + 1))
                if part == 0:
                    nc.scalar.copy(k_hi[:, 0:K_CUT], k_next[:, 0:K_CUT]).then_inc(k_hi_done, 1)
                else:
                    nc.scalar.copy(k_hi[:, K_CUT:S], k_next[:, K_CUT:S])
                    nc.scalar.copy(k_hi[:, S:S + P], k_next[:, 0:P]).then_inc(k_hi_done, 1)

            def v_high(half):
                nc.scalar.copy(v_hi[:, 4 * half:4 * half + 4, :], v_next[:, 4 * half:4 * half + 4, :])\
                    .then_inc(v_hi_done, 1)

            def copy_vT(at, dn, half, bank):
                act.wait_ge(v_proj, at(2, 2 * dn + half + 1))
                if dn or half:
                    act.wait_ge(v_turned, at(2, 2 * dn + half))
                nc.scalar.copy(vT[:], bank).then_inc(vT_copied, 1)

            def copy_v(at, dn, half, bank):
                act.wait_ge(v_turned, at(2, 2 * dn + half + 1))
                if dn:
                    act.wait_ge(v_split, at(2, 2 * dn))
                nc.scalar.copy(v_next[:, 4 * half:4 * half + 4, :].rearrange("p k d -> p (k d)"), bank)\
                    .then_inc(v_copied, 1)

            def exp(at, dn, j, h):
                act.wait_ge(negated, at(T * H, dn * T * H + j * H + h + 1))
                nc.scalar.activation(p[:, j % 2, h, :], p[:, j % 2, h, :], ACT.Exp, bias=neg_max[:, j % 2, h:h + 1],
                                     scale=SCALE, accum_out=row_sum[:, j % 2, h:h + 1]).then_inc(exp_done, 1)

            def p_high(at, g, t):
                k = g * TV + t
                act.wait_ge(pT_ready, at(T * TV, k + 1))
                nc.scalar.copy(pT_hi[:, k % 2, :], ps_t[:, k % 2, :]).then_inc(pT_hi_done, 1)

            def o_high(at, g):
                act.wait_ge(o_ready, at(8, g))
                nc.scalar.copy(oT_hi[:], ps_o[:]).then_inc(oT_hi_done, 1)

            def tile(g, at, last, first=False):
                dn, j = following(g)
                more = not (last and g == T - 1)
                if not first:
                    o_high(at, g)
                p_high(at, g, 0)
                p_high(at, g, 1)
                if first:
                    q_high(at, 4, 1, 0)
                if not last:
                    if g in (2, 3):
                        swap(at, rope_slot(g - 1, "k", last), ps_m)
                    elif g in (4, 6):
                        copy_vT(at, 1, (g - 4) // 2, ps_m[:])
                    elif g in (5, 7):
                        copy_v(at, 1, (g - 5) // 2, ps_m[:])
                if g == 0 and not first:
                    v_high(1)
                for h in range(H):
                    if more:
                        exp(at, dn, j, h)
                    if not last and g == 6 and h == 2:
                        act.wait_ge(s_ready, at(T * H, T * H))
                        k_high(at, rope_slot(2, "k", last), 0)
                    p_high(at, g, 2 + h)
                q = not last or g <= 4
                if q:
                    r = rope_slot(g, "q", last)
                    swap(at, r, ps_m)
                p_high(at, g, 6)
                if not last and g == 7:
                    act.wait_ge(v_used, at(1, 1))
                    act.wait_ge(v_copied, at(2, 4))
                    v_high(0)
                if not last and g == 6:
                    k_high(at, rope_slot(2, "k", last), 1)
                if q:
                    q_high(at, r, ((g + 3) // 2) % 4, (g + 1) % 2)
            act.wait_ge(built, 9)
            with act.Fori(0, B) as b:
                at0 = counts(act, b, 0)(0)
                for c in range(1, C):
                    act.wait_ge(xt_in[c], b * 16 + 16)
                    nc.scalar.copy(x_hi[:, c, :], x_raw[:, c * S:(c + 1) * S]).then_inc(xh_done, 1)
                swap(at0, 0, ps_m)
                swap(at0, 1, ps_o)
                swap(at0, 2, ps_t[:, 0, :])
                k_high(at0, 1, 0)
                q_high(at0, 2, 0, 0)
                swap(at0, 3, ps_t[:, 1, :])
                k_high(at0, 1, 1)
                q_high(at0, 3, 0, 1)
                copy_vT(at0, 0, 0, ps_m[:])
                for h in range(H):
                    exp(at0, 0, 0, h)
                copy_v(at0, 0, 0, ps_t[:, 0, :])
                copy_vT(at0, 0, 1, ps_o[:])
                act.wait_ge(v_copied, at0(2, 1))
                v_high(0)
                swap(at0, 4, ps_m)
                copy_v(at0, 0, 1, ps_o[:])
                act.wait_ge(v_copied, at0(2, 2))
                v_high(1)
                tiles_of_batch(act, b, tile)

                o_high(counts(act, b, KV)(0), 0)
                act.wait_ge(f_stat, b * T + T - 1)
                nc.scalar.activation(std[:, 0:T - 1], mv[:, 0:T - 1, 1], ACT.Sqrt, bias=eps, scale=1.0)\
                    .then_inc(f_std, 1)

                def h_copy(i):
                    act.wait_ge(f_h, b * T + i + 1)
                    nc.scalar.copy(h_sb[:, i, :], (ps_o, ps_m)[i % 2][:, 0:R + NEXP]).then_inc(f_copied, 1)

                for i in range(T):
                    act.wait_ge(f_turned, b * T + i + 1)
                    nc.scalar.copy(x_hi[:, :, i * P:(i + 1) * P],
                                   ps_t[:, i % 2, :].rearrange("p (c t) -> p c t", c=C)).then_inc(f_hi, 1)
                    if i == 1:
                        act.wait_ge(f_stat, b * T + T)
                        nc.scalar.activation(std[:, T - 1:T], mv[:, T - 1, 1:2], ACT.Sqrt, bias=eps, scale=1.0)\
                            .then_inc(f_std, 1)
                    if i >= 1:
                        h_copy(i - 1)
                h_copy(T - 1)

                def std_2(i):
                    act.wait_ge(f_stat2, b * T + i + 1)
                    nc.scalar.activation(std2[:, i:i + 1], mv2[:, i, 1:2], ACT.Sqrt, bias=eps, scale=1.0)\
                        .then_inc(f_std2, 1)

                def finish(i):
                    act.wait_ge(f_mean2, b * T + i + 1)
                    nc.scalar.activation(y[:, i, :], y[:, i, :], ACT.Identity, bias=mv2[:, i, 0:1],
                                         scale=rstd2[:, i:i + 1]).then_inc(f_done, 1)
                    act.wait_ge(f_done, b * T + i + 1)
                    act.dma_start(out[bass.ds(b, 1), i * P:(i + 1) * P, :].rearrange("a s e -> (a s) e"),
                                  y[:, i, :]).then_inc(stored, 16)

                for i in range(T):
                    act.wait_ge(f_gT, b * T + i + 1)
                    if i >= 2:
                        act.wait_ge(f_out, b * T + i - 1)
                    nc.scalar.copy(oT_hi[:, (i % 2) * P:(i % 2 + 1) * P], ps_t[:, i % 2, 0:P]).then_inc(f_gT_hi, 1)
                    if i >= 2:
                        std_2(i - 2)
                    if i >= 3:
                        finish(i - 3)
                std_2(T - 2)
                finish(T - 3)
                std_2(T - 1)
                finish(T - 2)
                finish(T - 1)

        @block.vector
        def _(dve):
            def times_cos(at, r, q_before, bank, t0, tokens, heads):
                dst = first_rope[r][0] if r < 5 else rope_a[:]
                if r >= 5:
                    dve.wait_ge(rope_sum, at(10, r))
                    dve.wait_ge(q_split, at(8, q_before))
                dve.wait_ge(proj_ready, at(10, r + 1))
                cs = cos_sb[:, t0:t0 + tokens].unsqueeze(1).broadcast_to([P, heads, tokens])
                nc.vector.tensor_tensor(dst.rearrange("p (h t) -> p h t", h=heads),
                                        bank.rearrange("p (h t) -> p h t", h=heads), cs, ALU.mult)\
                    .then_inc(rope_cos, 1)

            def rotated(at, r, dst):
                dve.wait_ge(rope_cos, at(10, r + 1))
                dve.wait_ge(rope_sin, at(10, r + 1))
                a, s = first_rope[r] if r < 5 else (rope_a[:], rope_s[:])
                nc.vector.tensor_tensor(dst, a, s, ALU.add).then_inc(rope_sum, 1)

            def q_low(at, qn, r, pair, half):
                dve.wait_ge(rope_sum, at(10, r + 1))
                dve.wait_ge(q_hi_done, at(8, qn + 1))
                sl = (slice(None), pair % 2, slice(2 * half, 2 * half + 2), slice(None))
                src = first_rope[r][0] if r < 5 else rope_a[:]
                nc.vector.tensor_tensor(q_lo[sl], src.rearrange("p (h t) -> p h t", h=2),
                                        q_hi[sl].bitcast(F32), ALU.subtract).then_inc(q_split, 1)

            def k_low(at, dn, r, part):
                dve.wait_ge(rope_sum, at(10, r + 1))
                dve.wait_ge(k_hi_done, at(2, 2 * dn + part + 1))
                a, z_ = (0, K_CUT) if part == 0 else (K_CUT, S)
                if part:
                    nc.vector.tensor_tensor(k_lo[:, S:S + P], k_next[:, 0:P], k_hi[:, S:S + P].bitcast(F32),
                                            ALU.subtract)
                nc.vector.tensor_tensor(k_lo[:, a:z_], k_next[:, a:z_], k_hi[:, a:z_].bitcast(F32), ALU.subtract)\
                    .then_inc(k_split, 1)

            def v_low(at, dn, half):
                dve.wait_ge(v_hi_done, at(2, 2 * dn + half + 1))
                sl = (slice(None), slice(4 * half, 4 * half + 4), slice(None))
                nc.vector.tensor_tensor(v_lo[sl], v_next[sl], v_hi[sl].bitcast(F32), ALU.subtract)\
                    .then_inc(v_split, 1)

            def mask_max(at, dn, j, h):
                start = score_chunks(j, T)[0]
                mask = mask_end[:, 0:KEYS] if j == 0 else mask_end[:, P:KEYS + P] if j == T - 1 else mask_mid[:]
                u = dn * T * H + j * H + h
                wait_apart(dve, s_ready, at(T * H, u + 1))
                nc.vector.tensor_tensor_reduce(p[:, j % 2, h, :], ps_s[:, h % 2, start:start + KEYS], mask, 1.0,
                                               MASKED, ALU.add, ALU.max,
                                               row_max[:, j % 2, h:h + 1]).then_inc(masked, 1)
                dve.wait_ge(masked, at(T * H, u + 1))
                nc.vector.tensor_scalar(neg_max[:, j % 2, h:h + 1], row_max[:, j % 2, h:h + 1], -SCALE, None,
                                        ALU.mult).then_inc(negated, 1)

            def invert(at, dn, j, h):
                dve.wait_ge(exp_done, at(T * H, dn * T * H + j * H + h + 1))
                nc.vector.reciprocal(row_inv[:, j % 2, h:h + 1], row_sum[:, j % 2, h:h + 1]).then_inc(inverted, 1)

            def p_low(at, g, t):
                k = g * TV + t
                dve.wait_ge(pT_hi_done, at(T * TV, k + 1))
                nc.vector.tensor_tensor(pT_lo[:, k % 2, :], ps_t[:, k % 2, :], pT_hi[:, k % 2, :].bitcast(F32),
                                        ALU.subtract).then_inc(pT_split, 1)

            def add_y(at, g):
                i = (g - 1) % T
                dve.wait_ge(wo_ready, at(8, g))
                nc.vector.tensor_tensor(y[:, i, :], ps_m[:], y[:, i, :], ALU.add).then_inc(y_added, 1)

            def o_low(at, g):
                dve.wait_ge(oT_hi_done, at(8, g))
                nc.vector.tensor_tensor(oT_lo[:], ps_o[:], oT_hi[:].bitcast(F32), ALU.subtract)\
                    .then_inc(oT_split, 1)

            def tile(g, at, last, first=False):
                dn, j = following(g)
                more = not (last and g == T - 1)
                keys = not last and g in (2, 3)
                if keys:
                    rk_ = rope_slot(g - 1, "k", last)
                    times_cos(at, rk_, 3 + g, ps_m[:], (g - 2) * 512, 512, 1)
                if not first:
                    o_low(at, g)
                p_low(at, g, 0)
                if more:
                    mask_max(at, dn, j, 0)
                if first:
                    rotated(at, 4, first_rope[4][0])
                p_low(at, g, 1)
                if g == 0 and not first:
                    v_low(at, 0, 1)
                if more:
                    mask_max(at, dn, j, 1)
                if first:
                    q_low(at, 2, 4, 1, 0)
                p_low(at, g, 2)
                if more:
                    invert(at, dn, j, 0)
                    if first:
                        dve.wait_ge(q_split, at(8, 3))
                    mask_max(at, dn, j, 2)
                if not first:
                    add_y(at, g)
                    if last and g >= 2:
                        dve.wait_ge(y_added, at(8, g - 1))
                        tile_stats(g - 2)
                if more:
                    invert(at, dn, j, 1)
                p_low(at, g, 3)
                if more:
                    mask_max(at, dn, j, 3)
                    invert(at, dn, j, 2)
                if keys:
                    rotated(at, rk_, k_next[:, (g - 2) * 512:(g - 1) * 512])
                p_low(at, g, 4)
                q = not last or g <= 4
                pair, half = ((g + 3) // 2) % 4, (g + 1) % 2
                if q:
                    r = rope_slot(g, "q", last)
                    times_cos(at, r, 3 + g, ps_m[:], pair * 2 * P, 2 * P, 2)
                if more:
                    invert(at, dn, j, 3)
                p_low(at, g, 5)
                if not last and g == 6:
                    k_low(at, 1, rope_slot(2, "k", last), 0)
                p_low(at, g, 6)
                if q:
                    rotated(at, r, rope_a[:])
                if not last and g == 7:
                    v_low(at, 1, 0)
                if not last and g == 6:
                    k_low(at, 1, rope_slot(2, "k", last), 1)
                if q:
                    q_low(at, 3 + g, r, pair, half)
            def tile_stats(i):
                nc.vector.bn_stats(stats[:, i, :], y[:, i, :]).then_inc(f_stat1, 1)

            LINKS = NEXP + 14

            def feed_forward(b):
                links = [0]

                def step(ins):
                    links[0] += 1
                    ins.then_inc(chain, 1)
                    wait_apart(dve, chain, b * LINKS + links[0])

                atL = counts(dve, b, KV)(0)
                dve.wait_ge(y_added, atL(8, -1))
                tile_stats(T - 2)
                wait_apart(dve, f_stat1, b * T + T - 1)
                for i in range(T - 1):
                    nc.vector.bn_aggr(mv[:, i, :], stats[:, i, :]).then_inc(f_stat, 1)
                o_low(atL, 0)
                dve.wait_ge(f_std, 2 * b + 1)
                step(nc.vector.reciprocal(rstd[:, 0:T - 1], std[:, 0:T - 1]))

                def normalise(i):
                    nc.vector.tensor_scalar(y[:, i, :], y[:, i, :], mv[:, i, 0:1], rstd[:, i:i + 1], ALU.subtract,
                                            ALU.mult).then_inc(f_norm, 1)

                normalise(0)
                normalise(1)
                add_y(atL, 0)

                def x_low(i):
                    dve.wait_ge(f_hi, b * T + i + 1)
                    s = (slice(None), slice(None), slice(i * P, (i + 1) * P))
                    nc.vector.tensor_tensor(x_lo[s], ps_t[:, i % 2, :].rearrange("p (c t) -> p c t", c=C),
                                            x_hi[s].bitcast(F32), ALU.subtract).then_inc(f_lo, 1)

                x_low(0)
                dve.wait_ge(y_added, atL(8, 0))
                tile_stats(T - 1)
                wait_apart(dve, f_stat1, b * T + T)
                nc.vector.bn_aggr(mv[:, T - 1, :], stats[:, T - 1, :]).then_inc(f_stat, 1)
                for i in range(1, T):
                    if i == 2:
                        dve.wait_ge(f_std, 2 * b + 2)
                        step(nc.vector.reciprocal(rstd[:, T - 1:T], std[:, T - 1:T]))
                    if i + 1 < T:
                        normalise(i + 1)
                    x_low(i)

                def each(v):
                    return v.unsqueeze(1).broadcast_to([P, T, NEXP])

                def per_tile(v):
                    return v.unsqueeze(2).broadcast_to([P, T, NEXP])

                dve.wait_ge(f_copied, b * T + T)
                step(nc.vector.tensor_tensor(z[:], h_sb[:, :, R:R + NEXP], each(br), ALU.add))
                for i in range(T):
                    ins = nc.vector.max(zs[:, i, :], z[:, i, :])
                step(ins)
                step(nc.vector.tensor_copy(zc[:, :, 0:1], zs[:, :, 0:1]))
                for k in range(1, NEXP):
                    step(nc.vector.tensor_tensor(zc[:, :, k:k + 1], zc[:, :, k - 1:k], zs[:, :, k:k + 1], ALU.add))
                step(nc.vector.tensor_tensor(zk[:], zs[:], each(rank), ALU.mult))
                step(nc.vector.tensor_scalar(zk[:], zk[:], 1.0, None, ALU.add))
                step(nc.vector.tensor_tensor(zt[:], zk[:], zc[:], ALU.is_gt))
                step(nc.vector.tensor_reduce(kz, zt[:], AX.X, ALU.add))
                step(nc.vector.tensor_tensor(zt[:], each(rank), per_tile(kz), ALU.is_equal))
                step(nc.vector.tensor_tensor(zt[:], zt[:], zc[:], ALU.mult))
                nc.vector.reciprocal(rk, kz)
                step(nc.vector.tensor_reduce(tau, zt[:], AX.X, ALU.add))
                step(nc.vector.scalar_tensor_tensor(tau, tau, -1.0, rk, ALU.add, ALU.mult))
                step(nc.vector.tensor_tensor(wts[:], z[:], per_tile(tau), ALU.subtract))
                step(nc.vector.tensor_scalar(wts[:], wts[:], 0.0, None, ALU.max))
                assert links[0] == LINKS, links

                def gate(i):
                    if i >= 2:
                        dve.wait_ge(f_gT, b * T + i - 1)
                    nc.vector.tensor_tensor(gated[:, i % 2, :].rearrange("p (e r) -> p e r", e=NEXP),
                                            h_sb[:, i, 0:R].rearrange("p (e r) -> p e r", e=NEXP),
                                            wts[:, i, :].unsqueeze(2).broadcast_to([P, NEXP, RANK]),
                                            ALU.mult).then_inc(f_gated, 1)

                def gated_low(i):
                    dve.wait_ge(f_gT_hi, b * T + i + 1)
                    s = slice((i % 2) * P, (i % 2 + 1) * P)
                    nc.vector.tensor_tensor(oT_lo[:, s], ps_t[:, i % 2, 0:P], oT_hi[:, s].bitcast(F32),
                                            ALU.subtract).then_inc(f_gT_lo, 1)

                def add(i):
                    dve.wait_ge(f_out, b * T + i + 1)
                    dve.wait_ge(f_biased, b * T + i + 1)
                    nc.vector.tensor_tensor(y[:, i, :], ffn_bank(i), y[:, i, :], ALU.add)\
                        .then_inc(f_sum, 1)
                    dve.wait_ge(f_sum, b * T + i + 1)
                    nc.vector.bn_stats(stats[:, i, :], y[:, i, :]).then_inc(f_stats, 1)
                    wait_apart(dve, f_stats, b * T + i + 1)
                    nc.vector.bn_aggr(mv2[:, i, :], stats[:, i, :]).then_inc(f_stat2, 1)

                def scale_2(i):
                    dve.wait_ge(f_std2, b * T + i + 1)
                    nc.vector.reciprocal(rstd2[:, i:i + 1], std2[:, i:i + 1]).then_inc(f_rstd2, 1)
                    dve.wait_ge(f_rstd2, b * T + i + 1)
                    nc.vector.tensor_scalar(mv2[:, i, 0:1], mv2[:, i, 0:1], rstd2[:, i:i + 1], -1.0,
                                            ALU.mult, ALU.mult).then_inc(f_mean2, 1)

                gate(0)
                gate(1)
                gated_low(0)
                for i in range(T):
                    if i + 1 < T:
                        gated_low(i + 1)
                    if i + 2 < T:
                        gate(i + 2)
                    add(i)
                    if i >= 1:
                        scale_2(i - 1)
                scale_2(T - 1)

            dve.sem_inc(pT_split, CREDIT)
            dve.wait_ge(built, 9)
            dve.wait_ge(consts_in, 16 * 5)
            with dve.Fori(0, B) as b:
                at0 = counts(dve, b, 0)(0)
                wait_apart(dve, xt_in[0], b * 16 + 16)
                nc.vector.tensor_copy(x_hi[:, 0, :], x_raw[:, 0:S]).then_inc(x0_done, 1)
                for c in range(C):
                    if c == 0:
                        dve.wait_ge(x0_done, b + 1)
                    else:
                        dve.wait_ge(xh_done, b * (C - 1) + c)
                    nc.vector.tensor_tensor(x_lo[:, c, :], x_raw[:, c * S:(c + 1) * S], x_hi[:, c, :].bitcast(F32),
                                            ALU.subtract).then_inc(xl_done, 1)
                times_cos(at0, 0, 0, ps_m[:], 0, 512, 1)
                times_cos(at0, 1, 0, ps_o[:], 512, 512, 1)
                rotated(at0, 0, first_rope[0][0])
                times_cos(at0, 2, 0, ps_t[:, 0, :], 0, 2 * P, 2)
                rotated(at0, 1, first_rope[1][0])
                k_low(at0, 0, 1, 0)
                rotated(at0, 2, first_rope[2][0])
                times_cos(at0, 3, 0, ps_t[:, 1, :], 0, 2 * P, 2)
                q_low(at0, 0, 2, 0, 0)
                k_low(at0, 0, 1, 1)
                rotated(at0, 3, first_rope[3][0])
                q_low(at0, 1, 3, 0, 1)
                for h in range(H):
                    mask_max(at0, 0, 0, h)
                    if h:
                        invert(at0, 0, 0, h - 1)
                invert(at0, 0, 0, H - 1)
                v_low(at0, 0, 0)
                times_cos(at0, 4, 0, ps_m[:], 2 * P, 2 * P, 2)
                v_low(at0, 0, 1)
                dve.wait_ge(y_in, b * 16 + 16)
                tiles_of_batch(dve, b, tile)
                feed_forward(b)


def program(nc, ins, out_shape):
    args = [nc.dram_tensor(f"in_{k}", a.shape, mybir.dt.from_np(a.dtype), kind="ExternalInput").ap()
            for k, a in ins.items()]
    out = nc.dram_tensor("out", out_shape, F32, kind="ExternalOutput").ap()
    attention_ffn(nc, *args, out)


def kernel(**inputs):
    import numpy as np
    import concourse.bacc as bacc
    from concourse.bass_utils import run_bass_kernel_spmd

    a = {k: np.asarray(v) for k, v in inputs.items()}
    x, wq, wk, wv = (a["L0_attn_" + k] for k in ("hidden_states", "Wq", "Wk", "Wv"))
    B, S, E = x.shape
    D, KV = 128, wk.shape[0] // 128
    turned = lambda w: w.reshape(KV, w.shape[0] // KV, E).transpose(0, 2, 1)
    lora_a = a["L0_ffn_lora_A"]
    NEXP, _, RANK = lora_a.shape
    down = np.zeros((1, E, 2 * D), np.float32)
    down[0, :, 0:NEXP * RANK] = lora_a.transpose(1, 0, 2).reshape(E, NEXP * RANK)
    down[0, :, NEXP * RANK:NEXP * RANK + NEXP] = a["L0_ffn_W_router"].T
    exponent = (np.arange(0, D, 2, dtype=np.float32) / np.float32(D)).astype(np.float32)
    power = np.power(10000.0, exponent.astype(np.float64)).astype(np.float32)
    inverse = (np.float32(1.0) / power).astype(np.float32)
    angle = (np.arange(S, dtype=np.float32)[None, :] * inverse[:, None]).astype(np.float64)
    cos, sin = np.cos(angle).astype(np.float32), np.sin(angle).astype(np.float32)
    ins = {
        "xT": x.transpose(0, 2, 1),
        "x": x,
        "wqT": np.concatenate([turned(wq), a["L0_ffn_W_base"].T[None]], 0),
        "wkvT": np.concatenate([np.concatenate([turned(wk), turned(wv)], 2), down], 0),
        "woT": a["L0_attn_Wo"].T.reshape(KV, 4 * D, E),
        "loraB": a["L0_ffn_lora_B"].reshape(NEXP * RANK, E),
        "b_base": a["L0_ffn_b_base"],
        "b_router": a["L0_ffn_b_router"],
        "cosT": np.concatenate([cos, cos], 0),
        "sinT": np.concatenate([-sin, sin], 0),
        "ranks": np.arange(1, NEXP + 1, dtype=np.float32),
    }
    ins = {k: np.ascontiguousarray(v) for k, v in ins.items()}
    nc = bacc.Bacc("TRN2", target_bir_lowering=False, num_devices=1)
    program(nc, ins, x.shape)
    r = run_bass_kernel_spmd(nc, [{f"in_{k}": v for k, v in ins.items()}], core_ids=[0])
    return r.results[0]["out"]
```
